# Optimizing a Trainium2 kernel written in Bass

```python
import numpy as np
import jax
import jax.numpy as jnp

def _softmax(x, axis=-1):
    return jax.nn.softmax(x, axis=axis)

def _gelu(x):
    return jax.nn.gelu(x, approximate=True)

def _silu(x):
    return jax.nn.silu(x)

def _sigmoid(x):
    return jax.nn.sigmoid(x)

def _layernorm(x, axis=-1, eps=1e-05):
    m = jnp.mean(x, axis=axis, keepdims=True)
    v = jnp.var(x, axis=axis, keepdims=True)
    return (x - m) / jnp.sqrt(v + eps)

def _scatter_add(tgt, idx, src, axis=0):
    return tgt.at[idx].add(src)

def _segment_sum(src, seg, n):
    return jax.ops.segment_sum(src, seg, n)
kernel_name = 'mk_adj_preln_d2_adj_r2_f9cbfe'

def setup_inputs(seed: int=0):
    np.random.seed(seed)
    _w = jnp.asarray

    def _rec_inputs():
        import jax
        import jax.numpy as jnp
        _gk = jax.random.key(seed)
        x = -0.0002928 + 1 * jax.random.normal(jax.random.fold_in(_gk, 1), (2048, 512), jnp.float32)
        _w = (1.0 + jnp.arange(2048, dtype=jnp.float32)) ** (-0.5)
        _w = _w / _w.mean()
        _pij = jnp.clip(0.00195312 * _w[:, None] * _w[None, :], 0.0, 1.0)
        _a = jax.random.uniform(jax.random.fold_in(_gk, 2), (2048, 2048)) < _pij
        _af = _a.astype(jnp.float32)
        adj = _af
        return (x, adj)
    x, adj = _rec_inputs()

    def _L0_gnn_setup():
        import jax, jax.numpy as jnp
        import numpy as np
        N = 2048
        D_IN = 512
        H = 16
        DH = D_IN // H
        ALPHA = 0.2
        MASK_VAL = -65500.0
        key = jax.random.key(seed)
        ks = jax.random.split(key, 7)
        x = jax.random.normal(ks[0], (N, D_IN), dtype=jnp.float32)
        adj = jax.random.randint(ks[1], (N, N), 0, 2).astype(jnp.float32)
        s = 1.0 / np.sqrt(D_IN)
        W_seq = jax.random.normal(ks[2], (D_IN, D_IN), dtype=jnp.float32) * s
        a1 = jax.random.normal(ks[3], (DH,), dtype=jnp.float32) / np.sqrt(DH)
        a2 = jax.random.normal(ks[4], (DH,), dtype=jnp.float32) / np.sqrt(DH)
        W_out = jax.random.normal(ks[5], (D_IN, D_IN), dtype=jnp.float32) * s
        b_out = jax.random.normal(ks[6], (D_IN,), dtype=jnp.float32) * 0.01
        return {'x': x, 'adj': adj, 'W_seq': W_seq, 'a1': a1, 'a2': a2, 'W_out': W_out, 'b_out': b_out}
    _L0_gnn_all = _L0_gnn_setup()
    _L0_gnn_in = {k: v for k, v in _L0_gnn_all.items() if k in ('W_seq', 'a1', 'a2', 'W_out', 'b_out')}
    del _L0_gnn_all

    def _L1_gnn_setup():
        import jax, jax.numpy as jnp
        import numpy as np
        N = 4096
        D = 512

        def adjacent_mat(adj):
            adj = adj + jnp.eye(adj.shape[0], dtype=adj.dtype)
            deg = jnp.sum(adj, axis=1)
            dinv = jnp.where(deg > 0, deg ** (-0.5), 0.0).astype(adj.dtype)
            return dinv[:, None] * adj * dinv[None, :]
        key = jax.random.key(seed)
        k1, k2 = jax.random.split(key)
        x = jax.random.normal(k1, (N, D), dtype=jnp.float32)
        Coefficient2 = 1e-08 * jnp.ones((N, N), dtype=jnp.float32)
        A = jax.random.uniform(k2, (N, N), dtype=jnp.float32)
        return {'x': x, 'Coefficient2': Coefficient2, 'A': A}
    _L1_gnn_all = _L1_gnn_setup()
    _L1_gnn_in = {k: v for k, v in _L1_gnn_all.items() if k in ()}
    del _L1_gnn_all
    return {'x': x, 'adj': adj, 'L0_gnn_W_seq': _L0_gnn_in['W_seq'], 'L0_gnn_a1': _L0_gnn_in['a1'], 'L0_gnn_a2': _L0_gnn_in['a2'], 'L0_gnn_W_out': _L0_gnn_in['W_out'], 'L0_gnn_b_out': _L0_gnn_in['b_out']}

def reference(x, adj, L0_gnn_W_seq, L0_gnn_a1, L0_gnn_a2, L0_gnn_W_out, L0_gnn_b_out):
    import jax
    import jax.numpy as jnp

    def _L0_gnn_ref(x, adj, W_seq, a1, a2, W_out, b_out):
        import jax, jax.numpy as jnp
        import numpy as np
        N = 2048
        D_IN = 512
        H = 16
        DH = D_IN // H
        ALPHA = 0.2
        MASK_VAL = -65500.0
        seq = (x @ W_seq).reshape(N, H, DH)
        score1 = jnp.einsum('nhd,d->hn', seq, a1)
        score2 = jnp.einsum('nhd,d->hn', seq, a2)
        scores = score1[:, :, None] + score2[:, None, :]
        scores = jax.nn.leaky_relu(scores, negative_slope=ALPHA)
        scores = scores + (1.0 - adj)[None, :, :] * MASK_VAL
        attn = jax.nn.softmax(scores, axis=-1)
        hidden = jnp.einsum('hij,jhd->ihd', attn, seq).reshape(N, D_IN)
        hidden = hidden @ W_out + b_out
        return jax.nn.elu(hidden)

    def _L1_gnn_ref(x, Coefficient2, A):
        import jax, jax.numpy as jnp
        import numpy as np
        N = 4096
        D = 512

        def adjacent_mat(adj):
            adj = adj + jnp.eye(adj.shape[0], dtype=adj.dtype)
            deg = jnp.sum(adj, axis=1)
            dinv = jnp.where(deg > 0, deg ** (-0.5), 0.0).astype(adj.dtype)
            return dinv[:, None] * adj * dinv[None, :]
        A_c = jax.lax.stop_gradient(A)
        adj = adjacent_mat((A_c + A_c.T) * 0.5)
        y = Coefficient2 @ adj
        y = y @ x
        return y
    h = jnp.maximum(_layernorm(x, axis=-1), 0.0)
    x = x + _L0_gnn_ref(h, adj, L0_gnn_W_seq, L0_gnn_a1, L0_gnn_a2, L0_gnn_W_out, L0_gnn_b_out)
    h = jnp.maximum(_layernorm(x, axis=-1), 0.0)
    x = x + _L1_gnn_ref(h, adj, adj)
    return x

_drawn_inputs = setup_inputs


def setup_inputs(seed=0):
    import zlib

    import numpy as np

    out = dict(_drawn_inputs(seed))
    spreads = {}
    factors = {'L0_gnn_a1': 4.87, 'L0_gnn_b_out': 5.03}
    for name, (base, spread) in spreads.items():
        noise = np.random.default_rng([zlib.crc32(name.encode()), seed]).standard_normal(out[name].shape)
        drawn = base * np.exp(spread * noise) if base else spread * noise
        out[name] = jnp.asarray(drawn.astype(out[name].dtype))
    for name, factor in factors.items():
        out[name] = (out[name] * factor).astype(out[name].dtype)
    return out
```

```python
from contextlib import ExitStack

import concourse.bass as bass
from concourse import mybir

P = 128
F32 = mybir.dt.float32
BF16 = mybir.dt.bfloat16
F16 = mybir.dt.float16
FP8 = mybir.dt.float8e4
U32 = mybir.dt.uint32
U8 = mybir.dt.uint8
ALU = mybir.AluOpType
ACT = mybir.ActivationFunctionType
AX_X = mybir.AxisListType.X
ds = bass.ds


class Semaphores:

    def __init__(self, sem):
        self.settled = sem("settled")
        self.w_in = sem("w_in")
        self.a_in = sem("a_in")
        self.x_first = sem("x_first")
        self.x_rest = sem("x_rest")
        self.adj_in0 = sem("adj_in0")
        self.adj_in1 = sem("adj_in1")
        self.consts0 = sem("consts0")
        self.consts = sem("consts")
        self.wa_mul = sem("wa_mul")
        self.wa_red = sem("wa_red")
        self.st_done = sem("st_done")
        self.ag_done = sem("ag_done")
        self.var_ready = sem("var_ready")
        self.std_ready = sem("std_ready")
        self.rs_done = sem("rs_done")
        self.ln_ready = sem("ln_ready")
        self.h_ready = sem("h_ready")
        self.hT_ps = sem("hT_ps")
        self.hT_sb = sem("hT_sb")
        self.seq_ps = sem("seq_ps")
        self.seq_sb = sem("seq_sb")
        self.ones_col = sem("ones_col")
        self.adj_cast = sem("adj_cast")
        self.empty_done = sem("empty_done")
        self.adj_filled = sem("adj_filled")
        self.at_ps0 = sem("at_ps0")
        self.at_ps1 = sem("at_ps1")
        self.at_sb0 = sem("at_sb0")
        self.at_sb1 = sem("at_sb1")
        self.adj_read = sem("adj_read")
        self.col_ps = sem("col_ps")
        self.sT_ps = sem("sT_ps")
        self.sT_sb = sem("sT_sb")
        self.s12_ps = sem("s12_ps")
        self.s12_sb = sem("s12_sb")
        self.rows_sb = sem("rows_sb")
        self.rows_out = sem("rows_out")
        self.small = sem("small")
        self.cmax_ps = sem("cmax_ps")
        self.ne_cnt = sem("ne_cnt")
        self.v_ready = sem("v_ready")
        self.u_ready = sem("u_ready")
        self.cmp_ready = sem("cmp_ready")
        self.all_ready = sem("all_ready")
        self.row_in0 = sem("row_in0")
        self.row_in1 = sem("row_in1")
        self.bias_ready = sem("bias_ready")
        self.steps = sem("steps")
        self.m_dve = sem("m_dve")
        self.m_ready = sem("m_ready")
        self.n_ready = sem("n_ready")
        self.mask_used = sem("mask_used")
        self.acc_free = sem("acc_free")
        self.prep = sem("prep")
        self.vals_ready = sem("vals_ready")
        self.weighed = sem("weighed")
        self.summed = sem("summed")
        self.recip = sem("recip")
        self.hidden_ready = sem("hidden_ready")
        self.dinv_small = sem("dinv_small")
        self.dinv_sqrt = sem("dinv_sqrt")
        self.dinv_ready = sem("dinv_ready")
        self.wo_in = sem("wo_in")
        self.b_in = sem("b_in")
        self.xr_in0 = sem("xr_in0")
        self.xr_in1 = sem("xr_in1")
        self.diag_ready = sem("diag_ready")
        self.ne_ps = sem("ne_ps")
        self.ne_sb = sem("ne_sb")
        self.adj_true = sem("adj_true")
        self.hid_cp = sem("hid_cp")
        self.hid_ps = sem("hid_ps")
        self.hid_T = sem("hid_T")
        self.o_ps = sem("o_ps")
        self.t_ready = sem("t_ready")
        self.n_min = sem("n_min")
        self.p_ready = sem("p_ready")
        self.e_ready = sem("e_ready")
        self.q_ready = sem("q_ready")
        self.x1_ready = sem("x1_ready")
        self.ln2_st = sem("ln2_st")
        self.ln2_ag = sem("ln2_ag")
        self.ln2_var = sem("ln2_var")
        self.ln2_std = sem("ln2_std")
        self.ln2_small = sem("ln2_small")
        self.ln2_ready = sem("ln2_ready")
        self.xg_ready = sem("xg_ready")
        self.ghi = sem("ghi")
        self.glo = sem("glo")
        self.s_sum = sem("s_sum")
        self.s_ready = sem("s_ready")
        self.z_ps = sem("z_ps")
        self.z_cp = sem("z_cp")
        self.zhi = sem("zhi")
        self.zlo = sem("zlo")
        self.a_ready = sem("a_ready")
        self.y_ps = sem("y_ps")
        self.y_hi = sem("y_hi")
        self.y_sb = sem("y_sb")
        self.out_done0 = sem("out_done0")
        self.out_done1 = sem("out_done1")


def gat_gcn(nc, x, adj, w_seq, a1, a2, w_out, b_out, out):
    N, D = x.shape
    DH = a1.shape[0]
    H = D // DH
    NT = N // P
    KC = D // P
    G = 4
    NG = NT // G
    HALF = N // 2
    TU = NT // 2
    CJ = 4
    NCH = NT // CJ
    NPART = 3
    W33 = DH + 1
    SLOT = H * W33
    ALPHA = 0.2
    EPS = 1e-5
    BIG = 2.0 ** 90
    TINY = 2.0 ** -50
    G_SCALE = 2.0 ** 10
    Z_SCALE = 2.0 ** 5
    LO_SCALE = 2.0 ** 11
    ONE8 = 0x38
    DVE_JT = (3, 11)

    s1_dram = nc.dram_tensor("s1_rows", [H, N], F32, kind="Internal").ap()

    with ExitStack() as ctx:
        def sb(name, shape, dt):
            return ctx.enter_context(nc.sbuf_tensor(name, shape, dt))

        def sem(name):
            return ctx.enter_context(nc.semaphore(name))

        adj_t = sb("adj_t", [P, NT, N], FP8)
        adj_n = sb("adj_n", [P, NT, N], FP8)
        nodes = sb("nodes", [P, NT, SLOT], F32)
        wmat = sb("wmat", [P, KC, D], F32)
        masks = sb("masks", [P, 32768], FP8)
        vals = sb("vals", [P, 2 * NT * NPART * 2 * W33], BF16)
        rows = sb("rows", [P, 2, HALF], F32)
        work = sb("work", [P, 8192], F32)

        ident = sb("ident", [P, P], F32)
        ident_b = sb("ident_b", [P, P], BF16)
        ones_b = sb("ones_b", [P, P], BF16)
        zeros_b = sb("zeros_b", [P, NT], BF16)
        ones_p = sb("ones_p", [P, P], F32)
        ones_f = sb("ones_f", [2 * H, P], F32)
        a12 = sb("a12", [P, 2, DH], F32)
        w12 = sb("w12", [P, KC, 2 * H], F32)
        stats = sb("stats", [P, G, 6], F32)
        mv = sb("mv", [P, G, 2], F32)
        std = sb("std", [P, G], F32)
        rstd = sb("rstd", [P, NT], F32)
        nmr = sb("nmr", [P, NT], F32)
        rowsum = sb("rowsum", [P, NT], F32)
        empty = sb("empty", [P, NT], F32)
        colsum = sb("colsum", [P, NT], F32)
        dinv = sb("dinv", [P, NT], F32)
        dsum = sb("dsum", [P, NT], F32)
        st_grp = sb("st_grp", [2 * H, G * P], F32)
        s12 = sb("s12", [P, NT, 2 * H], F32)
        smax = sb("smax", [2 * H, 1], F32)
        dmax = sb("dmax", [2 * H, 2 * H], F32)
        cmax = sb("cmax", [P, H], F32)
        tdiff = sb("tdiff", [P, NT, H], F32)
        tsum = sb("tsum", [P, NT, H], F32)
        tmin = sb("tmin", [P, NT, H], F32)
        v2 = sb("v2", [P, NT, 2, H], F32)
        u2 = sb("u2", [P, NT, 2, H], F32)
        n_empty = sb("n_empty", [P, 1], F32)
        kall = sb("kall", [P, NT, H], F32)
        nall = sb("nall", [P, NT, H], F32)
        s2cmp = sb("s2cmp", [P, NT, H], F32)
        kbias = sb("kbias", [P, 2, NT], F32)
        negs2 = sb("negs2", [P, 2, NT], F32)
        rden = sb("rden", [P, 2, TU], F32)

        x_slot = nodes[:, :, 0:D]
        seq = nodes[:, :, :].rearrange("p t (h c) -> p t h c", c=W33)
        stage = masks[:, :].bitcast(F32)
        adj_in = stage[:, 0:2 * N].rearrange("p (b n) -> p b n", b=2)
        adj_b = stage[:, 2 * N:3 * N].bitcast(BF16).rearrange("p (b n) -> p b n", b=2)
        h_buf = stage[:, 3 * N:3 * N + 2 * D].rearrange("p (b n) -> p b n", b=2)
        adj_t8 = adj_t[:, :, :].bitcast(U8)
        adj_n8 = adj_n[:, :, :].bitcast(U8)
        mM = masks[:, 0:16384].rearrange("p (c j i) -> p c j i", c=NCH, j=CJ)
        mN = masks[:, 16384:32768].rearrange("p (c j i) -> p c j i", c=NCH, j=CJ)
        g_parts = masks[:, :].bitcast(F16).rearrange("p (t s n) -> p t s n", s=2, n=D)
        wa_tmp = vals[:, 0:2 * KC * D].bitcast(F32).rearrange("p (k h d) -> p k h d", k=KC, d=DH)
        vp = vals[:, :].rearrange("p (b t q s c) -> p b t q s c", b=2, t=NT, q=NPART, s=2)
        s_buf = vals[:, 0:2 * N].rearrange("p (b t i) -> p b t i", b=2, t=NT)
        a_buf = vals[:, 0:N].bitcast(FP8).rearrange("p (b t i) -> p b t i", b=2, t=NT)
        z_tmp = vals[:, 2 * N:2 * N + 4 * D].bitcast(F32).rearrange("p (b n) -> p b n", b=2)
        o_tmp = vals[:, N:N + 4 * D].bitcast(F32).rearrange("p (b n) -> p b n", b=2)
        st_rows = rows[0:2 * H, :, :].rearrange("p b n -> p (b n)")
        hT = work[:, 0:KC * G * P].rearrange("p (k n) -> p k n", k=KC)
        R0, R1 = NT * 2 * W33, 2 * NT * 2 * W33
        r0 = work[:, 0:R0].rearrange("p (t s c) -> p t s c", t=NT, s=2)
        r1 = work[:, R0:R1].rearrange("p (t s c) -> p t s c", t=NT, s=2)
        red = work[:, R1:R1 + 2 * TU * 2 * W33].rearrange("p (b t c) -> p b t c", b=2, t=TU)
        fin = work[:, R1 + 2 * TU * 2 * W33:R1 + 3 * TU * 2 * W33].rearrange("p (t c) -> p t c", t=TU)

        def pair(n):
            return work[:, 2 * D * n:2 * D * n + 2 * D].rearrange("p (b n) -> p b n", b=2)
        hid, tbuf, nbuf, xr, xb, hT2 = (pair(n) for n in range(6))
        b_row = work[:, 12 * D:13 * D]
        ne_row = work[:, 13 * D:14 * D].bitcast(FP8)
        z_parts = work[:, :].bitcast(F16).rearrange("p (t s n) -> p t s n", s=2, n=D)
        diag = vals[:, 2 * N:3 * N].rearrange("p (t c) -> p t c", t=NT)

        ps = ctx.enter_context(nc.psum_tensor("ps", [P, 8, 512], F32))
        ps_adj = [ps[:, 4 + b, :].bitcast(BF16).rearrange("p (t i) -> p t i", i=P) for b in range(2)]
        acc = [ps[:, 4 * b:4 * b + 4, :].rearrange("p b (t c) -> p (b t) c", t=2) for b in range(2)]

        s = Semaphores(sem)

        def settle(eng):
            eng.sem_inc(s.settled, 1)

        def start_rings(eng, *names):
            for name in names:
                eng.sem_inc(name, 2)

        block = ctx.enter_context(nc.Block())

        @block.sync
        def _(sp):
            x_t = x.rearrange("(g t p) n -> g p t n", t=G, p=P)
            adj_tiles = adj.rearrange("(t p) n -> t p n", p=P)
            sp.dma_start(x_slot[:, 0:G, :], x_t[0]).then_inc(s.x_first, 16)
            sp.dma_start(wmat[:, :, :], w_seq.rearrange("(k p) n -> p k n", p=P)).then_inc(s.w_in, 16)
            sp.dma_start(a12[:, 0, :], a1.rearrange("(a d) -> a d", a=1).partition_broadcast(P)).then_inc(s.a_in, 16)
            sp.dma_start(a12[:, 1, :], a2.rearrange("(a d) -> a d", a=1).partition_broadcast(P)).then_inc(s.a_in, 16)
            sp.dma_start(adj_in[:, 0, :], adj_tiles[0]).then_inc(s.adj_in0, 16)
            sp.dma_start(x_slot[:, G:2 * G, :], x_t[1]).then_inc(s.x_rest, 16)
            sp.dma_start(adj_in[:, 1, :], adj_tiles[1]).then_inc(s.adj_in1, 16)
            for g in range(2, NG):
                sp.dma_start(x_slot[:, g * G:(g + 1) * G, :], x_t[g]).then_inc(s.x_rest, 16)
            with sp.Fori(0, NT // 2 - 1) as i:
                sp.wait_ge(s.adj_cast, 2 * i + 1)
                sp.dma_start(adj_in[:, 0, :], adj_tiles[ds(2 * i + 2, 1)].rearrange("a p n -> (a p) n")).then_inc(s.adj_in0, 16)
                sp.wait_ge(s.adj_cast, 2 * i + 2)
                sp.dma_start(adj_in[:, 1, :], adj_tiles[ds(2 * i + 3, 1)].rearrange("a p n -> (a p) n")).then_inc(s.adj_in1, 16)
            sp.wait_ge(s.rows_sb, NG)
            sp.wait_ge(s.small, 1)
            sp.dma_start(s1_dram, st_rows[0:H, :]).then_inc(s.rows_out, 16)
            sp.wait_ge(s.rows_out, 16)
            sp.dma_start(rows[:, 0, :], s1_dram[0:1, 0:HALF].partition_broadcast(P)).then_inc(s.row_in0, 16)
            sp.dma_start(rows[:, 1, :], s1_dram[0:1, HALF:N].partition_broadcast(P)).then_inc(s.row_in1, 16)
            sp.wait_ge(s.seq_ps, NT)
            sp.dma_start(wmat[:, :, :], w_out.rearrange("(k p) n -> p k n", p=P)).then_inc(s.wo_in, 16)
            with sp.Fori(0, H - 1) as h:
                for ih in range(2):
                    sp.wait_ge(s.steps, 2 * NCH * h + NCH * (ih + 1))
                    sp.wait_ge(s.m_ready, 2 * NCH * h + NCH * (ih + 1))
                    sp.dma_start(rows[:, ih, :], s1_dram[ds(h + 1, 1), ih * HALF:(ih + 1) * HALF].partition_broadcast(P))\
                        .then_inc(s.row_in0 if ih == 0 else s.row_in1, 16)
            sp.wait_ge(s.hidden_ready, 2 * H)
            sp.dma_start(b_row, b_out.rearrange("(a d) -> a d", a=1).partition_broadcast(P)).then_inc(s.b_in, 16)
            x_tiles = x.rearrange("(t p) n -> t p n", p=P)
            sp.dma_start(xr[:, 0, :], x_tiles[0]).then_inc(s.xr_in0, 16)
            sp.dma_start(xr[:, 1, :], x_tiles[1]).then_inc(s.xr_in1, 16)
            with sp.Fori(0, NT // 2 - 1) as i:
                sp.wait_ge(s.x1_ready, 2 * i + 1)
                sp.dma_start(xr[:, 0, :], x_tiles[ds(2 * i + 2, 1)].rearrange("a p n -> (a p) n")).then_inc(s.xr_in0, 16)
                sp.wait_ge(s.x1_ready, 2 * i + 2)
                sp.dma_start(xr[:, 1, :], x_tiles[ds(2 * i + 3, 1)].rearrange("a p n -> (a p) n")).then_inc(s.xr_in1, 16)
            sp.sem_inc(s.out_done0, 16)
            sp.sem_inc(s.out_done1, 16)
            out_tiles = out.rearrange("(t p) n -> t p n", p=P)
            with sp.Fori(0, NT // 2) as i:
                for b in range(2):
                    sp.wait_ge(s.y_sb, 2 * i + b + 3)
                    sp.dma_start(out_tiles[ds(2 * i + b, 1)].rearrange("a p n -> (a p) n"), o_tmp[:, b, :])\
                        .then_inc((s.out_done0, s.out_done1)[b], 16)
            sp.wait_ge(s.out_done0, 8 * NT + 16)
            sp.wait_ge(s.out_done1, 8 * NT + 16)

        @block.gpsimd
        def _(pool):
            nc.gpsimd.memset(ident[:, :], 0.0).then_inc(s.consts0, 1)
            nc.gpsimd.memset(ones_b[:, :], 1.0).then_inc(s.consts, 1)
            nc.gpsimd.memset(ones_f[:, :], 1.0).then_inc(s.consts, 1)
            nc.gpsimd.memset(ones_p[:, :], 1.0).then_inc(s.consts, 1)
            nc.gpsimd.memset(zeros_b[:, :], 0.0).then_inc(s.consts, 1)
            pool.wait_ge(s.consts0, 1)
            nc.gpsimd.affine_select(out=ident[:, :], in_=ident[:, :], compare_op=ALU.not_equal, fill=1.0, base=0,
                                    pattern=[[-1, P]], channel_multiplier=1).then_inc(s.consts, 1)
            pool.wait_ge(s.consts, 5)
            nc.gpsimd.tensor_copy(ident_b[:, :], ident[:, :]).then_inc(s.consts, 1)
            pool.wait_ge(s.w_in, 16)
            pool.wait_ge(s.a_in, 32)
            for n in range(2):
                if n:
                    pool.wait_ge(s.wa_red, n)
                nc.gpsimd.tensor_tensor(wa_tmp, wmat[:, :, :].rearrange("p k (h d) -> p k h d", d=DH),
                                        a12[:, n, :].unsqueeze(1).unsqueeze(1).broadcast_to([P, KC, H, DH]),
                                        ALU.mult).then_inc(s.wa_mul, 1)
            pool.wait_ge(s.h_ready, NT)
            nc.gpsimd.memset(seq[:, :, :, DH:W33], 1.0).then_inc(s.ones_col, 1)

            def prep(h, b):
                nc.gpsimd.tensor_copy(kbias[:, b, :], kall[:, :, ds(h, 1)].rearrange("p t a -> p (t a)"))
                nc.gpsimd.tensor_copy(negs2[:, b, :], nall[:, :, ds(h, 1)].rearrange("p t a -> p (t a)"))\
                    .then_inc(s.bias_ready, 1)
                for side in range(2):
                    last = nc.gpsimd.tensor_tensor(
                        r0[:, :, side, :], seq[:, :, ds(h, 1), :].rearrange("p t a c -> p t (a c)"),
                        v2[:, :, side, ds(h, 1)].broadcast_to([P, NT, W33]), ALU.mult)
                last.then_inc(s.prep, 1)
                pool.wait_ge(s.prep, 4 * h + 1)
                settle(pool)
                nc.gpsimd.tensor_copy(vp[:, b, :, 0, :, :], r0).then_inc(s.prep, 1)
                pool.wait_ge(s.prep, 4 * h + 2)
                nc.gpsimd.tensor_tensor(r1, r0, vp[:, b, :, 0, :, :], ALU.subtract).then_inc(s.prep, 1)
                pool.wait_ge(s.prep, 4 * h + 3)
                settle(pool)
                nc.gpsimd.tensor_copy(vp[:, b, :, 1, :, :], r1).then_inc(s.prep, 1)
                pool.wait_ge(s.prep, 4 * h + 4)
                nc.gpsimd.tensor_tensor(vp[:, b, :, 2, :, :], r1, vp[:, b, :, 1, :, :], ALU.subtract)\
                    .then_inc(s.vals_ready, 1)

            def finish_unit(h, ih):
                u = 2 * h + ih
                t0 = ih * TU
                pool.wait_ge(s.acc_free, u + 3)
                settle(pool)
                for side in range(2):
                    last = nc.gpsimd.tensor_tensor(
                        red[:, ih, :, side * W33:(side + 1) * W33], red[:, ih, :, side * W33:(side + 1) * W33],
                        u2[:, t0:t0 + TU, side, ds(h, 1)].broadcast_to([P, TU, W33]), ALU.mult)
                last.then_inc(s.weighed, 1)
                pool.wait_ge(s.weighed, u + 1)
                nc.gpsimd.tensor_tensor(fin[:, :, 0:W33], red[:, ih, :, 0:W33], red[:, ih, :, W33:2 * W33],
                                        ALU.add).then_inc(s.summed, 1)
                pool.wait_ge(s.recip, u + 1)
                settle(pool)
                nc.gpsimd.tensor_tensor(
                    seq[:, t0:t0 + TU, ds(h, 1), 0:DH].rearrange("p t a c -> p t (a c)"), fin[:, :, 0:DH],
                    rden[:, ih, :].unsqueeze(2).broadcast_to([P, TU, DH]), ALU.mult).then_inc(s.hidden_ready, 1)

            def head(h, b, last=False):
                if not last:
                    pool.wait_ge(s.mask_used, NCH * (2 * h + 1))
                    pool.wait_ge(s.vals_ready, h + 1)
                    settle(pool)
                    prep(h + 1, 1 - b)
                for ih in range(2):
                    finish_unit(h, ih)

            pool.wait_ge(s.seq_sb, NT + 2)
            pool.wait_ge(s.ones_col, 1)
            pool.wait_ge(s.all_ready, 2)
            pool.wait_ge(s.v_ready, 2)
            pool.wait_ge(s.sT_ps, NG)
            prep(0, 0)
            pool.wait_ge(s.u_ready, 2)
            with pool.Fori(0, H // 2 - 1) as hp:
                head(2 * hp, 0)
                head(2 * hp + 1, 1)
            head(H - 2, 0)
            head(H - 1, 1, last=True)

            start_rings(pool, s.ghi)
            with pool.Fori(0, NG) as g:
                for k in range(G):
                    b = k % 2
                    t = G * g + k
                    pool.wait_ge(s.t_ready, t + 3)
                    settle(pool)
                    nc.gpsimd.tensor_scalar(nbuf[:, b, :], tbuf[:, b, :], 0.0, None, ALU.min).then_inc(s.n_min, 1)
                    pool.wait_ge(s.n_min, t + 1)
                    settle(pool)
                    nc.gpsimd.tensor_scalar(tbuf[:, b, :], tbuf[:, b, :], 0.0, -1.0, ALU.max, ALU.add)\
                        .then_inc(s.p_ready, 1)
                for k in range(G):
                    t = G * g + k
                    pool.wait_ge(s.xg_ready, t + 1)
                    settle(pool)
                    nc.gpsimd.tensor_copy(g_parts[:, ds(t, 1), 0, :].rearrange("p a n -> p (a n)"), xb[:, k % 2, :])\
                        .then_inc(s.ghi, 1)

        @block.scalar
        def _(act):
            def sqrt_var(g):
                act.wait_ge(s.var_ready, g + 1)
                nc.scalar.activation(std[:, :], mv[:, :, 1], ACT.Sqrt).then_inc(s.std_ready, 1)

            def relu_tile(t, b):
                nc.scalar.activation(h_buf[:, b, :], x_slot[:, ds(t, 1), :].rearrange("p a n -> p (a n)"), ACT.Relu,
                                     bias=nmr[:, ds(t, 1)], scale=rstd[:, ds(t, 1)]).then_inc(s.h_ready, 1)

            def tiles(g, last):
                for k in range(G):
                    t = G * g + k
                    b = k % 2
                    act.wait_ge(s.adj_in0 if b == 0 else s.adj_in1, 16 * (2 * g + k // 2) + 16)
                    settle(act)
                    nc.scalar.activation(adj_n8[:, ds(t, 1), :].rearrange("p a n -> p (a n)"), adj_in[:, b, :], ACT.Copy,
                                         scale=float(ONE8), accum_out=rowsum[:, ds(t, 1)]).then_inc(s.adj_cast, 1)
                    if not (last and k == G - 1):
                        act.wait_ge(s.ln_ready, g + 1 if k < G - 1 else g + 2)
                        act.wait_ge(s.hT_ps, t + 2)
                        settle(act)
                        relu_tile(t + 1, 1 - b)
                    act.wait_ge(s.seq_ps, t + 1)
                    settle(act)
                    nc.scalar.activation(seq[:, ds(t, 1), :, 0:DH].rearrange("p a h c -> p (a h) c"),
                                         ps[:, 2 + b, :].rearrange("p (h c) -> p h c", c=DH), ACT.Copy)\
                        .then_inc(s.seq_sb, 1)
                    act.wait_ge(s.at_ps1, t + 3)
                    settle(act)
                    nc.scalar.activation(adj_t8[:, NT // 2:NT, ds(P * t, P)], ps_adj[1], ACT.Copy, scale=float(ONE8))\
                        .then_inc(s.at_sb1, 1)

            start_rings(act, s.seq_sb, s.at_sb1)
            sqrt_var(0)
            act.wait_ge(s.ln_ready, 1)
            relu_tile(0, 0)
            with act.Fori(0, NG - 1) as g:
                sqrt_var(g + 1)
                tiles(g, False)
            tiles(NG - 1, True)

            act.wait_ge(s.dinv_small, 4)
            nc.scalar.activation(dsum[:, :], colsum[:, :], ACT.Sqrt).then_inc(s.dinv_sqrt, 1)
            act.wait_ge(s.small, 5)
            nc.scalar.activation(v2[:, :, 0, :], tdiff[:, :, :], ACT.Exp).then_inc(s.v_ready, 1)
            nc.scalar.activation(v2[:, :, 1, :], tdiff[:, :, :], ACT.Exp, scale=ALPHA).then_inc(s.v_ready, 1)
            act.wait_ge(s.small, 7)
            nc.scalar.activation(u2[:, :, 0, :], tmin[:, :, :], ACT.Exp, scale=1.0 - ALPHA).then_inc(s.u_ready, 1)
            nc.scalar.activation(u2[:, :, 1, :], tsum[:, :, :], ACT.Exp, scale=ALPHA - 1.0).then_inc(s.u_ready, 1)

            def unit(h, b, ih):
                act.wait_ge(s.row_in0 if ih == 0 else s.row_in1, 16 * h + 16)
                act.wait_ge(s.bias_ready, h + 1)
                for c in range(NCH):
                    act.wait_ge(s.mask_used, 2 * NCH * h + NCH * ih + c + 1)
                    settle(act)
                    todo = [k for k in range(CJ) if c * CJ + k not in DVE_JT]
                    for k in todo:
                        step = nc.scalar.activation(mM[:, c, k, :], rows[:, ih, :], ACT.Sigmoid,
                                                    bias=kbias[:, b, c * CJ + k:c * CJ + k + 1], scale=BIG,
                                                    saturate=False)
                    step.then_inc(s.steps, 1)

            with act.Fori(0, H // 2) as hp:
                for b in range(2):
                    for ih in range(2):
                        unit(2 * hp + b, b, ih)

            for n in range(4):
                act.wait_ge(s.ne_ps, n + 1)
                nc.scalar.activation(ne_row[:, n * 512:(n + 1) * 512], ps[:, 4 + n, :], ACT.Copy, saturate=False).then_inc(s.ne_sb, 1)

            def hidden_T(t, k):
                b = k % 2
                act.wait_ge(s.hid_ps, t + 1)
                settle(act)
                nc.scalar.activation(hid[:, b, :].rearrange("p (h c) -> p h c", c=DH),
                                     seq[:, ds(t, 1), :, 0:DH].rearrange("p a h c -> p (a h) c"), ACT.Copy)\
                    .then_inc(s.hid_cp, 1)
                act.wait_ge(s.hid_ps, t + 3)
                act.wait_ge(s.o_ps, t + 1)
                nc.scalar.activation(hT2[:, b, :], ps[:, b, :], ACT.Copy).then_inc(s.hid_T, 1)

            def out_group(g, last):
                for k in range(G):
                    b = k % 2
                    t = G * g + k
                    if not (last and k == G - 1):
                        hidden_T(t + 1, k + 1)
                    act.wait_ge(s.n_min, t + 1)
                    nc.scalar.activation(nbuf[:, b, :], nbuf[:, b, :], ACT.Exp).then_inc(s.e_ready, 1)
                act.wait_ge(s.ln2_var, g + 1)
                nc.scalar.activation(std[:, :], mv[:, :, 1], ACT.Sqrt).then_inc(s.ln2_std, 1)
                act.wait_ge(s.ln2_ready, g + 1)
                for k in range(G):
                    t = G * g + k
                    act.wait_ge(s.ghi, t + 1)
                    act.wait_ge(s.glo, t + 1)
                    settle(act)
                    nc.scalar.activation(xb[:, k % 2, :], x_slot[:, ds(t, 1), :].rearrange("p a n -> p (a n)"),
                                         ACT.Relu, bias=nmr[:, ds(t, 1)], scale=rstd[:, ds(t, 1)])\
                        .then_inc(s.xg_ready, 1)

            start_rings(act, s.hid_T, s.z_cp)
            act.wait_ge(s.hidden_ready, 2 * H)
            hidden_T(0, 0)
            with act.Fori(0, NG - 1) as g:
                out_group(g, False)
            out_group(NG - 1, True)
            with act.Fori(0, NT // 2) as i:
                for b in range(2):
                    t = 2 * i + b
                    act.wait_ge(s.z_ps, t + 3)
                    act.wait_ge(s.zlo, t + 1)
                    settle(act)
                    nc.scalar.activation(z_tmp[:, b, :], ps[:, b, :], ACT.Copy, scale=dsum[:, ds(t, 1)])\
                        .then_inc(s.z_cp, 1)

        @block.tensor
        def _(pe):
            def transpose_h(t, k):
                pe.wait_ge(s.h_ready, t + 1)
                for c in range(KC):
                    last = nc.tensor.transpose(ps[:, k % 2, c * P:(c + 1) * P], h_buf[:, k % 2, c * P:(c + 1) * P],
                                               ident[:, :])
                last.then_inc(s.hT_ps, 1)

            def tiles(g, last):
                for k in range(G):
                    t = G * g + k
                    b = k % 2
                    if not (last and k == G - 1):
                        transpose_h(t + 1, k + 1)
                    pe.wait_ge(s.hT_sb, t + 1)
                    pe.wait_ge(s.seq_sb, t + 1)
                    for c in range(KC):
                        mm = nc.tensor.matmul(ps[:, 2 + b, :], hT[:, c, k * P:(k + 1) * P], wmat[:, c, :],
                                              start=(c == 0), stop=(c == KC - 1))
                    mm.then_inc(s.seq_ps, 1)
                    if k == G - 1:
                        pe.wait_ge(s.wa_red, 2)
                        pe.wait_ge(s.s12_sb, g + 2)
                        for c in range(KC):
                            mm = nc.tensor.matmul(ps[0:2 * H, 6, :], w12[:, c, :], hT[:, c, :],
                                                  start=(c == 0), stop=(c == KC - 1))
                        mm.then_inc(s.sT_ps, 1)
                    pe.wait_ge(s.adj_filled, t + 1)
                    for half in range(2):
                        pe.wait_ge((s.at_sb0, s.at_sb1)[half], t + 2)
                        for j in range(NT // 2):
                            jt = half * (NT // 2) + j
                            tr = nc.tensor.transpose(ps_adj[half][:, j, :], adj_b[:, b, jt * P:(jt + 1) * P],
                                                     ident_b[:, :])
                        if half == 0:
                            tr.then_inc(s.at_ps0, 1)
                    tr.then_inc(s.at_ps1, 1)
                    for j in range(NT):
                        mm = nc.tensor.matmul(ps[:, 7, j:j + 1],
                                              adj_b[:, b, j * P:(j + 1) * P],
                                              ones_b[:, 0:1], start=False, stop=False, skip_group_check=True)
                    mm.then_inc(s.adj_read, 1)
                pe.wait_ge(s.sT_sb, g + 1)
                settle(pe)
                for k in range(G):
                    tr = nc.tensor.transpose(ps[:, 6, k * 2 * H:(k + 1) * 2 * H], st_grp[:, k * P:(k + 1) * P],
                                             ident[0:2 * H, 0:2 * H])
                tr.then_inc(s.s12_ps, 1)

            start_rings(pe, s.hT_ps, s.at_ps1, s.adj_read)
            pe.wait_ge(s.consts, 6)
            nc.tensor.matmul(ps[:, 7, 0:NT], ones_b[:, :], zeros_b[:, :], start=True, stop=False,
                             skip_group_check=True).then_inc(s.col_ps, 1)
            pe.wait_ge(s.w_in, 16)
            transpose_h(0, 0)
            with pe.Fori(0, NG - 1) as g:
                tiles(g, False)
            tiles(NG - 1, True)
            pe.wait_ge(s.small, 2)
            pe.wait_ge(s.s12_sb, NG + 2)
            nc.tensor.matmul(ps[:, 6, 0:H], ones_f[:, :], dmax[:, H:2 * H], start=True, stop=True)\
                .then_inc(s.cmax_ps, 1)
            nc.tensor.matmul(ps[:, 6, H:H + NT], ones_p[:, :], empty[:, :], start=True, stop=True)\
                .then_inc(s.ne_cnt, 1)
            pe.wait_ge(s.small, 3)
            pe.wait_ge(s.dinv_small, 3)
            pe.sem_inc(s.mask_used, NCH)
            pe.sem_inc(s.acc_free, 2)

            def unit(h, b, ih):
                u = 2 * h + ih
                pe.wait_ge(s.vals_ready, h + 1)
                pe.wait_ge(s.acc_free, u + 1)
                for c in range(NCH):
                    q = NCH * u + c
                    pe.wait_ge(s.m_ready, q + 1)
                    settle(pe)
                    for k in range(CJ):
                        jt = c * CJ + k
                        for side in range(2):
                            if k == 0 and side == 1:
                                pe.wait_ge(s.n_ready, q + 1)
                                settle(pe)
                            mask = mN if side else mM
                            for t in range(TU):
                                mm = nc.tensor.matmul(
                                    acc[ih][:, t, 0:NPART * 2 * W33].rearrange("p (q s c) -> p q s c", q=NPART, s=2)[:, :, side, :],
                                    mask[:, c, k, t * P:(t + 1) * P], vp[:, b, jt, :, side, :],
                                    start=(jt == 0 and side == 0 and t % 2 == 0),
                                    stop=(jt == NT - 1), skip_group_check=True)
                    mm.then_inc(s.mask_used, 1)

            with pe.Fori(0, H // 2) as hp:
                for b in range(2):
                    for ih in range(2):
                        unit(2 * hp + b, b, ih)

            pe.wait_ge(s.acc_free, 2 * H + 2)
            pe.wait_ge(s.diag_ready, 1)
            for n in range(4):
                nc.tensor.matmul(ps[:, 4 + n, :], ones_b[:, :],
                                 diag.rearrange("p t c -> p (t c)")[:, n * 512:(n + 1) * 512],
                                 start=True, stop=True).then_inc(s.ne_ps, 1)
            start_rings(pe, s.hid_ps, s.o_ps, s.z_ps, s.y_ps)
            pe.wait_ge(s.wo_in, 16)
            def transpose_hidden(t, k):
                pe.wait_ge(s.hid_cp, t + 1)
                pe.wait_ge(s.hid_T, t + 1)
                for c in range(KC):
                    tr = nc.tensor.transpose(ps[:, k % 2, c * P:(c + 1) * P], hid[:, k % 2, c * P:(c + 1) * P],
                                             ident[:, :])
                tr.then_inc(s.hid_ps, 1)

            def out_group(g, last):
                for k in range(G):
                    b = k % 2
                    t = G * g + k
                    if not (last and k == G - 1):
                        transpose_hidden(t + 1, k + 1)
                    pe.wait_ge(s.hid_T, t + 3)
                    pe.wait_ge(s.t_ready, t + 1)
                    for c in range(KC):
                        mm = nc.tensor.matmul(ps[:, 2 + b, :], hT2[:, b, c * P:(c + 1) * P], wmat[:, c, :],
                                              start=(c == 0), stop=(c == KC - 1))
                    mm.then_inc(s.o_ps, 1)

            transpose_hidden(0, 0)
            with pe.Fori(0, NG - 1) as g:
                out_group(g, False)
            out_group(NG - 1, True)
            pe.wait_ge(s.ghi, NT + 2)
            pe.wait_ge(s.glo, NT + 2)
            with pe.Fori(0, NT // 2) as i:
                for b in range(2):
                    t = 2 * i + b
                    pe.wait_ge(s.s_ready, t + 1)
                    pe.wait_ge(s.z_cp, t + 1)
                    for jt in range(NT):
                        for part in range(2):
                            mm = nc.tensor.matmul(ps[:, b, :], s_buf[:, b, jt, :], g_parts[:, jt, part, :],
                                                  start=(jt == 0 and part == 0), stop=(jt == NT - 1 and part == 1))
                    mm.then_inc(s.z_ps, 1)
            pe.wait_ge(s.zhi, NT)
            pe.wait_ge(s.zlo, NT + 2)
            with pe.Fori(0, NT // 2) as i:
                for b in range(2):
                    t = 2 * i + b
                    pe.wait_ge(s.a_ready, t + 1)
                    pe.wait_ge(s.y_sb, t + 1)
                    settle(pe)
                    for jt in range(NT):
                        for part in range(2):
                            mm = nc.tensor.matmul(ps[:, 2 + 2 * b + part, :], a_buf[:, b, jt, :],
                                                  z_parts[:, jt, part, :], start=(jt == 0), stop=(jt == NT - 1))
                    mm.then_inc(s.y_ps, 1)

        @block.vector
        def _(dve):
            def norm_stats(g):
                for k in range(G):
                    t = G * g + k
                    st = nc.vector.bn_stats(stats[:, k, :],
                                            x_slot[:, ds(t, 1), :].rearrange("p a n -> p (a n)"))
                st.then_inc(s.st_done, 1)
                dve.wait_ge(s.st_done, g + 1)
                settle(dve)
                for k in range(G):
                    ag = nc.vector.bn_aggr(mv[:, k, :], stats[:, k, :])
                ag.then_inc(s.ag_done, 1)
                dve.wait_ge(s.ag_done, g + 1)
                nc.vector.tensor_scalar(mv[:, :, 1], mv[:, :, 1], EPS, None, ALU.add)\
                    .then_inc(s.var_ready, 1)
                dve.wait_ge(s.std_ready, g + 1)
                settle(dve)
                nc.vector.reciprocal(rstd[:, ds(G * g, G)], std[:, :]).then_inc(s.rs_done, 1)
                dve.wait_ge(s.rs_done, g + 1)
                nc.vector.scalar_tensor_tensor(out=nmr[:, ds(G * g, G)], in0=mv[:, :, 0], scalar=-1.0,
                                               in1=rstd[:, ds(G * g, G)], op0=ALU.mult, op1=ALU.mult)\
                    .then_inc(s.ln_ready, 1)

            def copy_hT(t, k):
                dve.wait_ge(s.hT_ps, t + 3)
                nc.vector.tensor_copy(hT[:, :, (k % G) * P:(k % G + 1) * P],
                                      ps[:, k % 2, :].rearrange("p (c n) -> p c n", c=KC)).then_inc(s.hT_sb, 1)

            def tiles(g, last):
                for k in range(G):
                    t = G * g + k
                    b = k % 2
                    dve.wait_ge(s.adj_cast, t + 1)
                    nc.vector.tensor_scalar(empty[:, ds(t, 1)], rowsum[:, ds(t, 1)], 0.0, None, ALU.is_equal)\
                        .then_inc(s.empty_done, 1)
                    dve.wait_ge(s.empty_done, t + 1)
                    dve.wait_ge(s.adj_read, t + 1)
                    nc.vector.tensor_scalar(adj_b[:, b, :], adj_n8[:, ds(t, 1), :].rearrange("p a n -> p (a n)"),
                                            1.0 / ONE8, empty[:, ds(t, 1)], ALU.mult, ALU.max).then_inc(s.adj_filled, 1)
                    if k == G - 1 and not last:
                        dve.wait_ge(s.sT_ps, g + 1)
                    if not (last and k == G - 1):
                        copy_hT(t + 1, k + 1)
                    if k == G - 1:
                        dve.wait_ge(s.sT_ps, g + 1)
                        nc.vector.tensor_copy(st_grp[:, :], ps[0:2 * H, 6, :]).then_inc(s.sT_sb, 1)
                        dve.wait_ge(s.sT_sb, g + 1)
                        nc.vector.tensor_scalar(st_rows[:, ds(G * P * g, G * P)].bitcast(U32), st_grp[:, :].bitcast(U32),
                                                0xFFFFFFFE, None, ALU.bitwise_and).then_inc(s.rows_sb, 1)
                    dve.wait_ge(s.at_ps0, t + 1)
                    nc.vector.tensor_scalar(adj_t8[:, 0:NT // 2, ds(P * t, P)], ps_adj[0], float(ONE8), None, ALU.mult)\
                        .then_inc(s.at_sb0, 1)
                dve.wait_ge(s.s12_ps, g + 1)
                nc.vector.tensor_copy(s12[:, ds(G * g, G), :],
                                      ps[:, 6, 0:G * 2 * H].rearrange("p (t c) -> p t c", t=G)).then_inc(s.s12_sb, 1)

            start_rings(dve, s.at_sb0, s.s12_sb)
            dve.wait_ge(s.x_first, 16)
            norm_stats(0)
            for n in range(2):
                dve.wait_ge(s.wa_mul, n + 1)
                nc.vector.reduce_sum(w12[:, :, n * H:(n + 1) * H], wa_tmp, AX_X).then_inc(s.wa_red, 1)
            copy_hT(0, 0)
            dve.wait_ge(s.x_rest, 16 * (NG - 1))
            with dve.Fori(0, NG - 1) as g:
                norm_stats(g + 1)
                tiles(g, False)
            tiles(NG - 1, True)

            dve.wait_ge(s.rows_sb, NG)
            nc.vector.reduce_max(smax[:, :], st_rows, AX_X).then_inc(s.small, 1)
            dve.wait_ge(s.small, 1)
            nc.vector.tensor_scalar(dmax[:, :], ident[0:2 * H, 0:2 * H], smax[:, 0:1], None, ALU.mult)\
                .then_inc(s.small, 1)
            dve.wait_ge(s.cmax_ps, 1)
            dve.wait_ge(s.ne_cnt, 1)
            nc.vector.tensor_copy(cmax[:, :], ps[:, 6, 0:H]).then_inc(s.small, 1)
            dve.wait_ge(s.small, 3)
            dve.wait_ge(s.s12_sb, NG + 2)
            c_all = cmax[:, :].unsqueeze(1).broadcast_to([P, NT, H])
            nc.vector.tensor_tensor(tdiff[:, :, :], s12[:, :, H:2 * H], c_all, ALU.subtract).then_inc(s.small, 1)
            nc.vector.tensor_tensor(tsum[:, :, :], s12[:, :, 0:H], c_all, ALU.add).then_inc(s.small, 1)
            dve.wait_ge(s.small, 5)
            nc.vector.tensor_scalar(tmin[:, :, :], tsum[:, :, :], 0.0, None, ALU.min).then_inc(s.small, 1)
            dve.wait_ge(s.small, 6)
            nc.vector.tensor_scalar(tsum[:, :, :], tsum[:, :, :], 0.0, None, ALU.max).then_inc(s.small, 1)
            nc.vector.tensor_scalar(s2cmp[:, :, :], s12[:, :, H:2 * H], TINY, None, ALU.add).then_inc(s.cmp_ready, 1)
            dve.wait_ge(s.cmp_ready, 1)
            nc.vector.tensor_scalar(s2cmp[:, :, :].bitcast(U32), s2cmp[:, :, :].bitcast(U32), 1, None, ALU.bitwise_or)\
                .then_inc(s.cmp_ready, 1)
            dve.wait_ge(s.cmp_ready, 2)
            nc.vector.tensor_scalar(kall[:, :, :], s2cmp[:, :, :], BIG, None, ALU.mult).then_inc(s.all_ready, 1)
            nc.vector.tensor_scalar(nall[:, :, :], s2cmp[:, :, :], -1.0, None, ALU.mult).then_inc(s.all_ready, 1)
            nc.vector.reduce_sum(n_empty[:, :], ps[:, 6, H:H + NT], AX_X).then_inc(s.dinv_small, 1)
            dve.wait_ge(s.dinv_small, 1)
            dve.wait_ge(s.adj_read, NT + 2)
            nc.vector.tensor_scalar(colsum[:, :], ps[:, 7, 0:NT], n_empty[:, 0:1], None, ALU.subtract)\
                .then_inc(s.dinv_small, 1)
            dve.wait_ge(s.dinv_small, 2)
            nc.vector.scalar_tensor_tensor(out=colsum[:, :], in0=rowsum[:, :], scalar=1.0 / ONE8, in1=colsum[:, :],
                                           op0=ALU.mult, op1=ALU.add).then_inc(s.dinv_small, 1)
            dve.wait_ge(s.dinv_small, 3)
            nc.vector.tensor_scalar(colsum[:, :], colsum[:, :], 0.5, 1.0, ALU.mult, ALU.add).then_inc(s.dinv_small, 1)
            dve.wait_ge(s.dinv_sqrt, 1)
            nc.vector.reciprocal(dinv[:, :], dsum[:, :]).then_inc(s.dinv_ready, 1)
            dve.wait_ge(s.dinv_ready, 1)
            nc.vector.tensor_scalar(dsum[:, :], dinv[:, :], 0.5 * Z_SCALE * LO_SCALE / (G_SCALE * ONE8), None, ALU.mult)\
                .then_inc(s.dinv_ready, 1)

            def unit(h, b, ih, u, first):
                dve.wait_ge(s.row_in0 if ih == 0 else s.row_in1, 16 * h + 16)
                dve.wait_ge(s.bias_ready, h + 1)
                for c in range(NCH):
                    q = NCH * u + c
                    adj_c = adj_t[:, c * CJ:(c + 1) * CJ, ih * HALF:(ih + 1) * HALF].bitcast(U32)
                    dve.wait_ge(s.mask_used, q + 1)
                    settle(dve)
                    for k in range(CJ):
                        if c * CJ + k in DVE_JT:
                            nc.vector.tensor_scalar(mM[:, c, k, :], rows[:, ih, :],
                                                    negs2[:, b, c * CJ + k:c * CJ + k + 1], None, ALU.is_gt,
                                                    saturate=False).then_inc(s.m_dve, 1)
                    dve.wait_ge(s.m_dve, len(DVE_JT) * u + sum(j < (c + 1) * CJ for j in DVE_JT))
                    dve.wait_ge(s.steps, q + 1)
                    nc.vector.tensor_tensor(mM[:, c, :, :].bitcast(U32), mM[:, c, :, :].bitcast(U32), adj_c,
                                            ALU.bitwise_and).then_inc(s.m_ready, 1)
                    dve.wait_ge(s.m_ready, q + 1)
                    nc.vector.tensor_tensor(mN[:, c, :, :].bitcast(U32), mM[:, c, :, :].bitcast(U32), adj_c,
                                            ALU.bitwise_xor).then_inc(s.n_ready, 1)
                    if c == 0 and not (first and b == 0):
                        divide_unit(u - 2, ih)
                if not (first and b == 0 and ih == 0):
                    reduce_unit(u - 1, 1 - ih)

            def reduce_unit(u, ih):
                dve.wait_ge(s.mask_used, NCH * (u + 2))
                if not isinstance(u, int) or u > 0:
                    dve.wait_ge(s.hidden_ready, u)
                nc.vector.reduce_sum(red[:, ih, :, :],
                                     acc[ih][:, :, 0:NPART * 2 * W33].rearrange("p t (q c) -> p t c q", q=NPART),
                                     AX_X).then_inc(s.acc_free, 1)

            def divide_unit(u, ih):
                dve.wait_ge(s.summed, u + 1)
                nc.vector.reciprocal(rden[:, ih, :], fin[:, :, DH]).then_inc(s.recip, 1)

            def pair_of_heads(hp, first):
                for b in range(2):
                    for ih in range(2):
                        unit(2 * hp + b, b, ih, 4 * hp + 2 * b + ih, first)

            pair_of_heads(0, True)
            with dve.Fori(1, H // 2) as hp:
                pair_of_heads(hp, False)
            U = 2 * H
            divide_unit(U - 2, 0)
            dve.wait_ge(s.mask_used, NCH * (U + 1))
            nc.vector.tensor_scalar(empty[:, :], empty[:, :], -1.0, 1.0, ALU.mult, ALU.add).then_inc(s.empty_done, 1)
            reduce_unit(U - 1, 1)
            divide_unit(U - 1, 1)
            dve.wait_ge(s.empty_done, NT + 1)
            nc.vector.tensor_tensor(diag, ident_b[:, :].unsqueeze(1).broadcast_to([P, NT, P]),
                                    empty[:, :].unsqueeze(2).broadcast_to([P, NT, P]), ALU.mult)\
                .then_inc(s.diag_ready, 1)

            def tile_of(buf, t):
                return buf[:, ds(t, 1), :].rearrange("p a n -> p (a n)")

            start_rings(dve, s.t_ready, s.glo)
            dve.wait_ge(s.b_in, 16)
            dve.wait_ge(s.ne_sb, 4)
            with dve.Fori(0, NG) as g:
                for k in range(G):
                    b = k % 2
                    t = G * g + k
                    dve.wait_ge(s.o_ps, t + 3)
                    nc.vector.tensor_tensor(tbuf[:, b, :], ps[:, 2 + b, :], b_row, ALU.add).then_inc(s.t_ready, 1)
                    nc.vector.tensor_tensor(tile_of(adj_t, t).bitcast(U32), tile_of(adj_t, t).bitcast(U32),
                                            ne_row.bitcast(U32), ALU.bitwise_and).then_inc(s.adj_true, 1)
                    dve.wait_ge(s.p_ready, t + 1)
                    dve.wait_ge(s.e_ready, t + 1)
                    nc.vector.tensor_tensor(nbuf[:, b, :], nbuf[:, b, :], tbuf[:, b, :], ALU.add).then_inc(s.q_ready, 1)
                    dve.wait_ge(s.q_ready, t + 1)
                    dve.wait_ge(s.xr_in0 if b == 0 else s.xr_in1, 16 * (2 * g + k // 2) + 16)
                    nc.vector.tensor_tensor(tile_of(x_slot, t), nbuf[:, b, :], xr[:, b, :], ALU.add)\
                        .then_inc(s.x1_ready, 1)
                    dve.wait_ge(s.x1_ready, t + 1)
                    settle(dve)
                    nc.vector.bn_stats(stats[:, k, :], tile_of(x_slot, t)).then_inc(s.ln2_st, 1)
                    dve.wait_ge(s.ln2_st, t + 1)
                    settle(dve)
                    nc.vector.bn_aggr(mv[:, k, :], stats[:, k, :]).then_inc(s.ln2_ag, 1)
                dve.wait_ge(s.ln2_ag, G * g + G)
                nc.vector.tensor_scalar(mv[:, :, 1], mv[:, :, 1], EPS, None, ALU.add)\
                    .then_inc(s.ln2_var, 1)
                dve.wait_ge(s.ln2_std, g + 1)
                settle(dve)
                nc.vector.reciprocal(rstd[:, ds(G * g, G)], std[:, :]).then_inc(s.ln2_small, 1)
                dve.wait_ge(s.ln2_small, 2 * g + 1)
                nc.vector.scalar_tensor_tensor(out=rstd[:, ds(G * g, G)], in0=rstd[:, ds(G * g, G)], scalar=G_SCALE,
                                               in1=dinv[:, ds(G * g, G)], op0=ALU.mult, op1=ALU.mult)\
                    .then_inc(s.ln2_small, 1)
                dve.wait_ge(s.ln2_small, 2 * g + 2)
                nc.vector.scalar_tensor_tensor(out=nmr[:, ds(G * g, G)], in0=mv[:, :, 0], scalar=-1.0,
                                               in1=rstd[:, ds(G * g, G)], op0=ALU.mult, op1=ALU.mult)\
                    .then_inc(s.ln2_ready, 1)
                for k in range(G):
                    t = G * g + k
                    dve.wait_ge(s.ghi, t + 3)
                    nc.vector.tensor_tensor(g_parts[:, ds(t, 1), 1, :].rearrange("p a n -> p (a n)"), xb[:, k % 2, :],
                                            g_parts[:, ds(t, 1), 0, :].rearrange("p a n -> p (a n)"), ALU.subtract)\
                        .then_inc(s.glo, 1)

            def build_s(t, b):
                dve.wait_ge(s.z_ps, t + 1)
                nc.vector.tensor_tensor(s_buf[:, b, :, :], adj_t8[:, :, ds(P * t, P)], adj_n8[:, :, ds(P * t, P)],
                                        ALU.add).then_inc(s.s_sum, 1)
                dve.wait_ge(s.s_sum, t + 1)
                nc.vector.scalar_tensor_tensor(out=tile_of(s_buf[:, b], t), in0=ident_b[:, :], scalar=2.0 * ONE8,
                                               in1=tile_of(s_buf[:, b], t), op0=ALU.mult, op1=ALU.add)\
                    .then_inc(s.s_ready, 1)

            def copy_a(t, b):
                dve.wait_ge(s.y_ps, t + 1)
                settle(dve)
                nc.vector.tensor_copy(a_buf[:, b, :, :].bitcast(U32), adj_t[:, :, :].bitcast(U32)[:, :, ds(P // 4 * t, P // 4)])\
                    .then_inc(s.a_ready, 1)

            def split_z(t, b):
                dve.wait_ge(s.z_cp, t + 3)
                nc.vector.tensor_scalar(z_parts[:, ds(t, 1), 0, :].rearrange("p a n -> p (a n)"), z_tmp[:, b, :],
                                        1.0 / LO_SCALE, None, ALU.mult).then_inc(s.zhi, 1)
                dve.wait_ge(s.zhi, t + 1)
                nc.vector.scalar_tensor_tensor(out=z_parts[:, ds(t, 1), 1, :].rearrange("p a n -> p (a n)"),
                                               in0=z_parts[:, ds(t, 1), 0, :].rearrange("p a n -> p (a n)"),
                                               scalar=-LO_SCALE, in1=z_tmp[:, b, :], op0=ALU.mult, op1=ALU.add)\
                    .then_inc(s.zlo, 1)

            dve.wait_ge(s.adj_true, NT)
            start_rings(dve, s.zlo, s.y_sb)
            build_s(0, 0)
            with dve.Fori(0, NT // 2 - 1) as i:
                for b in range(2):
                    build_s(2 * i + b + 1, 1 - b)
                    split_z(2 * i + b, b)
            build_s(NT - 1, 1)
            split_z(NT - 2, 0)
            split_z(NT - 1, 1)
            def finish_y(t, b, i):
                dve.wait_ge(s.y_ps, t + 3)
                dve.wait_ge((s.out_done0, s.out_done1)[b], 16 * i + 16)
                nc.vector.scalar_tensor_tensor(out=o_tmp[:, b, :], in0=ps[:, 2 + 2 * b, :], scalar=1.0 / Z_SCALE,
                                               in1=tile_of(x_slot, t), op0=ALU.mult, op1=ALU.add)\
                    .then_inc(s.y_hi, 1)
                dve.wait_ge(s.y_hi, t + 1)
                nc.vector.scalar_tensor_tensor(out=o_tmp[:, b, :], in0=ps[:, 3 + 2 * b, :],
                                               scalar=1.0 / (Z_SCALE * LO_SCALE), in1=o_tmp[:, b, :],
                                               op0=ALU.mult, op1=ALU.add).then_inc(s.y_sb, 1)

            dve.wait_ge(s.z_ps, NT + 2)
            copy_a(0, 0)
            with dve.Fori(0, NT // 2 - 1) as i:
                for b in range(2):
                    copy_a(2 * i + b + 1, 1 - b)
                    finish_y(2 * i + b, b, i)
            copy_a(NT - 1, 1)
            finish_y(NT - 2, 0, NT // 2 - 1)
            finish_y(NT - 1, 1, NT // 2 - 1)


_INS = ["x", "adj", "L0_gnn_W_seq", "L0_gnn_a1", "L0_gnn_a2", "L0_gnn_W_out", "L0_gnn_b_out"]


def kernel(**inputs):
    import numpy as np
    import concourse.bacc as bacc
    from concourse.bass_utils import run_bass_kernel_spmd

    nc = bacc.Bacc("TRN2", target_bir_lowering=False, num_devices=1)
    arrays, args = {}, []
    for name in _INS:
        a = np.ascontiguousarray(inputs[name])
        arrays[f"in_{name}"] = a
        args.append(nc.dram_tensor(f"in_{name}", a.shape, mybir.dt.from_np(a.dtype), kind="ExternalInput").ap())
    out = nc.dram_tensor("out", inputs["x"].shape, F32, kind="ExternalOutput").ap()
    gat_gcn(nc, *args, out)
    r = run_bass_kernel_spmd(nc, [arrays], core_ids=[0])
    return r.results[0]["out"]
```

```python
from contextlib import ExitStack

import concourse.bass as bass
from concourse import mybir

P = 128
F32 = mybir.dt.float32
BF16 = mybir.dt.bfloat16
F16 = mybir.dt.float16
FP8 = mybir.dt.float8e4
U32 = mybir.dt.uint32
U8 = mybir.dt.uint8
ALU = mybir.AluOpType
ACT = mybir.ActivationFunctionType
AX_X = mybir.AxisListType.X
ds = bass.ds


class Semaphores:

    def __init__(self, sem):
        self.settled = sem("settled")
        self.w_in = sem("w_in")
        self.a_in = sem("a_in")
        self.x_first = sem("x_first")
        self.x_second = sem("x_second")
        self.x_rest = sem("x_rest")
        self.adj_in0 = sem("adj_in0")
        self.adj_in1 = sem("adj_in1")
        self.consts0 = sem("consts0")
        self.consts = sem("consts")
        self.wa_mul = sem("wa_mul")
        self.wa_red = sem("wa_red")
        self.st_done = sem("st_done")
        self.ag_done = sem("ag_done")
        self.var_ready = sem("var_ready")
        self.std_ready = sem("std_ready")
        self.rs_done = sem("rs_done")
        self.ln_ready = sem("ln_ready")
        self.h_ready = sem("h_ready")
        self.hT_ps = sem("hT_ps")
        self.hT_sb = sem("hT_sb")
        self.seq_ps = sem("seq_ps")
        self.seq_sb = sem("seq_sb")
        self.ones_col = sem("ones_col")
        self.adj_cast = sem("adj_cast")
        self.empty_done = sem("empty_done")
        self.adj_filled = sem("adj_filled")
        self.at_ps0 = sem("at_ps0")
        self.at_ps1 = sem("at_ps1")
        self.at_sb0 = sem("at_sb0")
        self.at_sb1 = sem("at_sb1")
        self.adj_read = sem("adj_read")
        self.col_ps = sem("col_ps")
        self.sT_ps = sem("sT_ps")
        self.sT_sb = sem("sT_sb")
        self.gmax_done = sem("gmax_done")
        self.s12_ps = sem("s12_ps")
        self.s12_sb = sem("s12_sb")
        self.rows_sb = sem("rows_sb")
        self.rows_out = sem("rows_out")
        self.small = sem("small")
        self.cmax_ps = sem("cmax_ps")
        self.ne_cnt = sem("ne_cnt")
        self.v_ready = sem("v_ready")
        self.u_ready = sem("u_ready")
        self.cmp_ready = sem("cmp_ready")
        self.all_ready = sem("all_ready")
        self.row_in0 = sem("row_in0")
        self.row_in1 = sem("row_in1")
        self.bias_ready = sem("bias_ready")
        self.steps = sem("steps")
        self.m_dve = sem("m_dve")
        self.m_ready = sem("m_ready")
        self.n_ready = sem("n_ready")
        self.mask_used = sem("mask_used")
        self.acc_free = sem("acc_free")
        self.prep = sem("prep")
        self.vals_ready = sem("vals_ready")
        self.weighed = sem("weighed")
        self.summed = sem("summed")
        self.recip = sem("recip")
        self.hidden_ready = sem("hidden_ready")
        self.dinv_small = sem("dinv_small")
        self.dinv_sqrt = sem("dinv_sqrt")
        self.dinv_ready = sem("dinv_ready")
        self.wo_in = sem("wo_in")
        self.b_in = sem("b_in")
        self.xr_in0 = sem("xr_in0")
        self.xr_in1 = sem("xr_in1")
        self.diag_ready = sem("diag_ready")
        self.ne_ps = sem("ne_ps")
        self.ne_sb = sem("ne_sb")
        self.hid_cp = sem("hid_cp")
        self.hid_ps = sem("hid_ps")
        self.hid_T = sem("hid_T")
        self.o_ps = sem("o_ps")
        self.t_ready = sem("t_ready")
        self.e_ready = sem("e_ready")
        self.em_ready = sem("em_ready")
        self.q_ready = sem("q_ready")
        self.x1_ready = sem("x1_ready")
        self.ln2_st = sem("ln2_st")
        self.ln2_ag = sem("ln2_ag")
        self.ln2_var = sem("ln2_var")
        self.ln2_std = sem("ln2_std")
        self.ln2_small = sem("ln2_small")
        self.ln2_ready = sem("ln2_ready")
        self.xg_ready = sem("xg_ready")
        self.ghi = sem("ghi")
        self.glo = sem("glo")
        self.col_true = sem("col_true")
        self.s_sum = sem("s_sum")
        self.s_ready = sem("s_ready")
        self.z_ps = sem("z_ps")
        self.z_cp = sem("z_cp")
        self.zhi = sem("zhi")
        self.zlo = sem("zlo")
        self.a_ready = sem("a_ready")
        self.y_ps = sem("y_ps")
        self.y_hi = sem("y_hi")
        self.y_sb = sem("y_sb")
        self.out_done0 = sem("out_done0")
        self.out_done1 = sem("out_done1")


def gat_gcn(nc, x, adj, w_seq, a1, a2, w_out, b_out, out):
    N, D = x.shape
    DH = a1.shape[0]
    H = D // DH
    NT = N // P
    KC = D // P
    G = 4
    NG = NT // G
    HALF = N // 2
    TU = NT // 2
    CJ = 4
    NCH = NT // CJ
    NPART = 3
    W33 = DH + 1
    SLOT = H * W33
    ALPHA = 0.2
    EPS = 1e-5
    BIG = 2.0 ** 90
    TINY = 2.0 ** -50
    G_SCALE = 2.0 ** 10
    Z_SCALE = 2.0 ** 5
    LO_SCALE = 2.0 ** 11
    ONE8 = 0x38
    DVE_JT = ((3, 11), (3, 11))
    NORM_AT = ((), (0,), (1,), (2, 3))
    DVE_PER_HEAD = len(DVE_JT[0]) + len(DVE_JT[1])

    s1_dram = nc.dram_tensor("s1_rows", [H, N], F32, kind="Internal").ap()

    with ExitStack() as ctx:
        def sb(name, shape, dt):
            return ctx.enter_context(nc.sbuf_tensor(name, shape, dt))

        def sem(name):
            return ctx.enter_context(nc.semaphore(name))

        adj_t = sb("adj_t", [P, NT, N], FP8)
        adj_n = sb("adj_n", [P, NT, N], FP8)
        nodes = sb("nodes", [P, NT, SLOT], F32)
        wmat = sb("wmat", [P, KC, D], F32)
        masks = sb("masks", [P, 32768], FP8)
        small_bufs = sb("small_bufs", [P, 3 * N], BF16)
        rows = sb("rows", [P, 2, HALF], F32)
        work = sb("work", [P, 8192], F32)

        ident = sb("ident", [P, P], F32)
        ident_b = sb("ident_b", [P, P], BF16)
        ones_b = sb("ones_b", [P, P], BF16)
        zeros_b = sb("zeros_b", [P, NT], BF16)
        ones_p = sb("ones_p", [P, P], F32)
        ones_f = sb("ones_f", [2 * H, P], F32)
        a12 = sb("a12", [P, 2, DH], F32)
        w12 = sb("w12", [P, KC, 2 * H], F32)
        stats = sb("stats", [P, G, 6], F32)
        mv = sb("mv", [P, G, 2], F32)
        std = sb("std", [P, G], F32)
        rstd = sb("rstd", [P, NT], F32)
        nmr = sb("nmr", [P, NT], F32)
        rowsum = sb("rowsum", [P, NT], F32)
        empty = sb("empty", [P, NT], F32)
        colsum = sb("colsum", [P, NT], F32)
        dinv = sb("dinv", [P, NT], F32)
        dsum = sb("dsum", [P, NT], F32)
        b_row = sb("b_row", [P, D], F32)
        s_grp = sb("s_grp", [P, G, 2 * H], F32)
        s12 = sb("s12", [P, NT, 2 * H], F32)
        gmax = sb("gmax", [2 * H, NG], F32)
        smax = sb("smax", [2 * H, 1], F32)
        dmax = sb("dmax", [2 * H, 2 * H], F32)
        cmax = sb("cmax", [P, H], F32)
        tdiff = sb("tdiff", [P, NT, H], F32)
        tsum = sb("tsum", [P, NT, H], F32)
        tmin = sb("tmin", [P, NT, H], F32)
        v2 = sb("v2", [P, NT, 2, H], F32)
        u2 = sb("u2", [P, NT, 2, H], F32)
        n_empty = sb("n_empty", [P, 1], F32)
        kall = sb("kall", [P, NT, H], F32)
        nall = sb("nall", [P, NT, H], F32)
        s2cmp = sb("s2cmp", [P, NT, H], F32)
        kbias = sb("kbias", [P, 2, NT], F32)
        negs2 = sb("negs2", [P, 2, NT], F32)
        rden = sb("rden", [P, 2, TU], F32)

        x_slot = nodes[:, :, 0:D]
        seq = nodes[:, :, :].rearrange("p t (h c) -> p t h c", c=W33)
        stage = masks[:, :].bitcast(F32)
        adj_in = stage[:, 0:2 * N].rearrange("p (b n) -> p b n", b=2)
        adj_b = stage[:, 2 * N:3 * N].bitcast(BF16).rearrange("p (b n) -> p b n", b=2)
        h_buf = stage[:, 3 * N:3 * N + 2 * D].rearrange("p (b n) -> p b n", b=2)
        adj_t8 = adj_t[:, :, :].bitcast(U8)
        adj_n8 = adj_n[:, :, :].bitcast(U8)
        mM = masks[:, 0:16384].rearrange("p (c j i) -> p c j i", c=NCH, j=CJ)
        mN = masks[:, 16384:32768].rearrange("p (c j i) -> p c j i", c=NCH, j=CJ)
        g_parts = masks[:, :].bitcast(F16).rearrange("p (t s n) -> p t s n", s=2, n=D)
        wa_tmp = small_bufs[:, 0:2 * KC * D].bitcast(F32).rearrange("p (k h d) -> p k h d", k=KC, d=DH)
        s_buf = small_bufs[:, 0:2 * N].rearrange("p (b t i) -> p b t i", b=2, t=NT)
        a_buf = small_bufs[:, 0:N].bitcast(FP8).rearrange("p (b t i) -> p b t i", b=2, t=NT)
        z_tmp = small_bufs[:, 2 * N:2 * N + 4 * D].bitcast(F32).rearrange("p (b n) -> p b n", b=2)
        o_tmp = small_bufs[:, N:N + 4 * D].bitcast(F32).rearrange("p (b n) -> p b n", b=2)
        st_grp = b_row[0:2 * H, 0:G * P]
        st_rows = rows[0:2 * H, :, :].rearrange("p b n -> p (b n)")
        hT = work[:, 0:KC * G * P].rearrange("p (k n) -> p k n", k=KC)
        VALS = NPART * NT * 2 * W33
        parts = work[:, 0:2 * VALS].rearrange("p (b q t s c) -> p b q t s c", b=2, q=NPART, t=NT, s=2)
        halves = work[:, 0:2 * VALS].bitcast(BF16).rearrange("p (b q t s c w) -> p b q t s c w", b=2, q=NPART, t=NT,
                                                             s=2, w=2)
        rest = work[:, 2 * VALS:]
        red = rest[:, 0:2 * TU * 2 * W33].rearrange("p (b t s c) -> p b t s c", b=2, t=TU, s=2)
        fin = rest[:, 2 * TU * 2 * W33:3 * TU * 2 * W33].rearrange("p (t s c) -> p t s c", t=TU, s=2)[:, :, 0, :]

        def pair(n):
            return work[:, 2 * D * n:2 * D * n + 2 * D].rearrange("p (b n) -> p b n", b=2)
        hid, hT2, tbuf, nbuf, xr, xb = (pair(n) for n in range(6))
        ne_row = rows[:, 0, 0:N // 4].bitcast(FP8)
        col_buf = rows[:, 1, 0:N // 4].rearrange("p (t i) -> p t i", t=NT)
        z_parts = work[:, :].bitcast(F16).rearrange("p (t s n) -> p t s n", s=2, n=D)
        diag = small_bufs[:, 2 * N:3 * N].rearrange("p (t c) -> p t c", t=NT)

        ps = ctx.enter_context(nc.psum_tensor("ps", [P, 8, 512], F32))
        ps_adj = [ps[:, 4 + b, :].bitcast(BF16).rearrange("p (t i) -> p t i", i=P) for b in range(2)]
        acc = [ps[:, 4 * b:4 * b + 4, :].rearrange("p b (t c) -> p (b t) c", t=2) for b in range(2)]

        s = Semaphores(sem)

        def x_loads(t, b):
            return 8 * (t - b) + 16

        def settle(eng):
            eng.sem_inc(s.settled, 1)

        def start_rings(eng, *names):
            for name in names:
                eng.sem_inc(name, 2)

        block = ctx.enter_context(nc.Block())

        @block.sync
        def _(sp):
            x_t = x.rearrange("(g t p) n -> g p t n", t=G, p=P)
            adj_tiles = adj.rearrange("(t p) n -> t p n", p=P)
            sp.dma_start(x_slot[:, 0:G, :], x_t[0]).then_inc(s.x_first, 16)
            sp.dma_start(wmat[:, :, :], w_seq.rearrange("(k p) n -> p k n", p=P)).then_inc(s.w_in, 16)
            sp.dma_start(a12[:, 0, :], a1.rearrange("(a d) -> a d", a=1).partition_broadcast(P)).then_inc(s.a_in, 16)
            sp.dma_start(a12[:, 1, :], a2.rearrange("(a d) -> a d", a=1).partition_broadcast(P)).then_inc(s.a_in, 16)
            sp.dma_start(adj_in[:, 0, :], adj_tiles[0]).then_inc(s.adj_in0, 16)
            sp.dma_start(adj_in[:, 1, :], adj_tiles[1]).then_inc(s.adj_in1, 16)
            sp.dma_start(x_slot[:, G:2 * G, :], x_t[1]).then_inc(s.x_second, 16)

            def adj_pair(i):
                sp.wait_ge(s.adj_cast, 2 * i + 1)
                sp.dma_start(adj_in[:, 0, :], adj_tiles[ds(2 * i + 2, 1)].rearrange("a p n -> (a p) n"))\
                    .then_inc(s.adj_in0, 16)
                sp.wait_ge(s.adj_cast, 2 * i + 2)
                sp.dma_start(adj_in[:, 1, :], adj_tiles[ds(2 * i + 3, 1)].rearrange("a p n -> (a p) n"))\
                    .then_inc(s.adj_in1, 16)

            adj_pair(0)
            for g in range(2, NG):
                sp.dma_start(x_slot[:, g * G:(g + 1) * G, :], x_t[g]).then_inc(s.x_rest, 16)
            with sp.Fori(1, NT // 2 - 1) as i:
                adj_pair(i)
            sp.wait_ge(s.rows_sb, NG)
            sp.wait_ge(s.small, 1)
            sp.dma_start(s1_dram, st_rows[0:H, :]).then_inc(s.rows_out, 16)
            sp.wait_ge(s.rows_out, 16)
            sp.dma_start(rows[:, 0, :], s1_dram[0:1, 0:HALF].partition_broadcast(P)).then_inc(s.row_in0, 16)
            sp.dma_start(rows[:, 1, :], s1_dram[0:1, HALF:N].partition_broadcast(P)).then_inc(s.row_in1, 16)
            sp.wait_ge(s.seq_ps, NT)
            sp.dma_start(wmat[:, :, :], w_out.rearrange("(k p) n -> p k n", p=P)).then_inc(s.wo_in, 16)
            with sp.Fori(0, H - 1) as h:
                for ih in range(2):
                    sp.wait_ge(s.steps, 2 * NCH * h + NCH * (ih + 1))
                    sp.wait_ge(s.m_ready, 2 * NCH * h + NCH * (ih + 1))
                    sp.dma_start(rows[:, ih, :], s1_dram[ds(h + 1, 1), ih * HALF:(ih + 1) * HALF].partition_broadcast(P))\
                        .then_inc(s.row_in0 if ih == 0 else s.row_in1, 16)
            sp.wait_ge(s.mask_used, NCH * (2 * H + 1))
            sp.dma_start(b_row[:, :], b_out.rearrange("(a d) -> a d", a=1).partition_broadcast(P)).then_inc(s.b_in, 16)
            x_tiles = x.rearrange("(t p) n -> t p n", p=P)
            sp.dma_start(xr[:, 0, :], x_tiles[0]).then_inc(s.xr_in0, 16)
            sp.dma_start(xr[:, 1, :], x_tiles[1]).then_inc(s.xr_in1, 16)
            with sp.Fori(0, NT // 2 - 1) as i:
                sp.wait_ge(s.x1_ready, 2 * i + 1)
                sp.dma_start(xr[:, 0, :], x_tiles[ds(2 * i + 2, 1)].rearrange("a p n -> (a p) n")).then_inc(s.xr_in0, 16)
                sp.wait_ge(s.x1_ready, 2 * i + 2)
                sp.dma_start(xr[:, 1, :], x_tiles[ds(2 * i + 3, 1)].rearrange("a p n -> (a p) n")).then_inc(s.xr_in1, 16)
            sp.sem_inc(s.out_done0, 16)
            sp.sem_inc(s.out_done1, 16)
            out_tiles = out.rearrange("(t p) n -> t p n", p=P)
            with sp.Fori(0, NT // 2) as i:
                for b in range(2):
                    sp.wait_ge(s.y_sb, 2 * i + b + 3)
                    sp.dma_start(out_tiles[ds(2 * i + b, 1)].rearrange("a p n -> (a p) n"), o_tmp[:, b, :])\
                        .then_inc((s.out_done0, s.out_done1)[b], 16)
            sp.wait_ge(s.out_done0, 8 * NT + 16)
            sp.wait_ge(s.out_done1, 8 * NT + 16)

        @block.gpsimd
        def _(pool):
            nc.gpsimd.memset(ident[:, :], 0.0).then_inc(s.consts0, 1)
            nc.gpsimd.memset(ones_b[:, :], 1.0).then_inc(s.consts, 1)
            nc.gpsimd.memset(ones_f[:, :], 1.0).then_inc(s.consts, 1)
            nc.gpsimd.memset(ones_p[:, :], 1.0).then_inc(s.consts, 1)
            nc.gpsimd.memset(zeros_b[:, :], 0.0).then_inc(s.consts, 1)
            pool.wait_ge(s.consts0, 1)
            nc.gpsimd.affine_select(out=ident[:, :], in_=ident[:, :], compare_op=ALU.not_equal, fill=1.0, base=0,
                                    pattern=[[-1, P]], channel_multiplier=1).then_inc(s.consts, 1)
            pool.wait_ge(s.consts, 5)
            nc.gpsimd.tensor_copy(ident_b[:, :], ident[:, :]).then_inc(s.consts, 1)
            pool.wait_ge(s.w_in, 16)
            pool.wait_ge(s.a_in, 32)
            for n in range(2):
                if n:
                    pool.wait_ge(s.wa_red, n)
                nc.gpsimd.tensor_tensor(wa_tmp, wmat[:, :, :].rearrange("p k (h d) -> p k h d", d=DH),
                                        a12[:, n, :].unsqueeze(1).unsqueeze(1).broadcast_to([P, KC, H, DH]),
                                        ALU.mult).then_inc(s.wa_mul, 1)
            pool.wait_ge(s.h_ready, NT)
            nc.gpsimd.memset(seq[:, :, :, DH:W33], 1.0).then_inc(s.ones_col, 1)

            def finish_unit(h, ih):
                u = 2 * h + ih
                t0 = ih * TU
                pool.wait_ge(s.acc_free, u + 3)
                settle(pool)
                nc.gpsimd.tensor_tensor(
                    red[:, ih, :, :, :], red[:, ih, :, :, :],
                    u2[:, t0:t0 + TU, :, ds(h, 1)].broadcast_to([P, TU, 2, W33]), ALU.mult).then_inc(s.weighed, 1)
                pool.wait_ge(s.weighed, u + 1)
                nc.gpsimd.tensor_tensor(fin, red[:, ih, :, 0, :], red[:, ih, :, 1, :], ALU.add).then_inc(s.summed, 1)
                pool.wait_ge(s.recip, u + 1)
                settle(pool)
                nc.gpsimd.tensor_tensor(
                    seq[:, t0:t0 + TU, ds(h, 1), 0:DH].rearrange("p t a c -> p t (a c)"), fin[:, :, 0:DH],
                    rden[:, ih, :].unsqueeze(2).broadcast_to([P, TU, DH]), ALU.mult).then_inc(s.hidden_ready, 1)

            pool.wait_ge(s.u_ready, 2)
            with pool.Fori(0, H) as h:
                for ih in range(2):
                    finish_unit(h, ih)

            start_rings(pool, s.glo)

            def add_x(t, b):
                pool.wait_ge(s.q_ready, t + 1)
                pool.wait_ge(s.xr_in0 if b == 0 else s.xr_in1, x_loads(t, b))
                settle(pool)
                nc.gpsimd.tensor_tensor(x_slot[:, ds(t, 1), :].rearrange("p a n -> p (a n)"), nbuf[:, b, :],
                                        xr[:, b, :], ALU.add).then_inc(s.x1_ready, 1)

            def low_part(t, b):
                pool.wait_ge(s.ghi, t + 1)
                settle(pool)
                nc.gpsimd.tensor_tensor(g_parts[:, ds(t, 1), 1, :].rearrange("p a n -> p (a n)"), xb[:, b, :],
                                        g_parts[:, ds(t, 1), 0, :].rearrange("p a n -> p (a n)"), ALU.subtract)\
                    .then_inc(s.glo, 1)

            for k in range(G):
                add_x(k, k % 2)
            with pool.Fori(1, NG) as g:
                for k in range(G):
                    add_x(G * g + k, k % 2)
                    for n in NORM_AT[k]:
                        low_part(G * (g - 1) + n, n % 2)

        @block.scalar
        def _(act):
            def sqrt_var(g):
                act.wait_ge(s.var_ready, g + 1)
                nc.scalar.activation(std[:, :], mv[:, :, 1], ACT.Sqrt).then_inc(s.std_ready, 1)

            def relu_tile(t, b):
                nc.scalar.activation(h_buf[:, b, :], x_slot[:, ds(t, 1), :].rearrange("p a n -> p (a n)"), ACT.Relu,
                                     bias=nmr[:, ds(t, 1)], scale=rstd[:, ds(t, 1)]).then_inc(s.h_ready, 1)

            def cast_adj(t, b):
                act.wait_ge(s.adj_in0 if b == 0 else s.adj_in1, x_loads(t, b))
                settle(act)
                nc.scalar.activation(adj_n8[:, ds(t, 1), :].rearrange("p a n -> p (a n)"), adj_in[:, b, :], ACT.Copy,
                                     scale=float(ONE8), accum_out=rowsum[:, ds(t, 1)]).then_inc(s.adj_cast, 1)

            def tiles(g, last):
                for k in range(G):
                    t = G * g + k
                    b = k % 2
                    if not (last and k == G - 1):
                        cast_adj(t + 1, 1 - b)
                    if not (last and k >= G - 2):
                        act.wait_ge(s.ln_ready, g + (1 if k < G - 2 else 2))
                        act.wait_ge(s.hT_ps, t + 3)
                        settle(act)
                        relu_tile(t + 2, b)
                    if k == 1 and not last:
                        sqrt_var(g + 1)
                    act.wait_ge(s.seq_ps, t + 1)
                    settle(act)
                    nc.scalar.activation(seq[:, ds(t, 1), :, 0:DH].rearrange("p a h c -> p (a h) c"),
                                         ps[:, 2 + b, :].rearrange("p (h c) -> p h c", c=DH), ACT.Copy)\
                        .then_inc(s.seq_sb, 1)
                    act.wait_ge(s.at_ps1, t + 3)
                    settle(act)
                    nc.scalar.activation(adj_t8[:, NT // 2:NT, ds(P * t, P)], ps_adj[1], ACT.Copy, scale=float(ONE8))\
                        .then_inc(s.at_sb1, 1)

            start_rings(act, s.seq_sb, s.at_sb1)
            sqrt_var(0)
            act.wait_ge(s.ln_ready, 1)
            relu_tile(0, 0)
            relu_tile(1, 1)
            cast_adj(0, 0)
            with act.Fori(0, NG - 1) as g:
                tiles(g, False)
            tiles(NG - 1, True)

            act.wait_ge(s.small, 4)
            nc.scalar.activation(v2[:, :, 0, :], tdiff[:, :, :], ACT.Exp).then_inc(s.v_ready, 1)
            nc.scalar.activation(v2[:, :, 1, :], tdiff[:, :, :], ACT.Exp, scale=ALPHA).then_inc(s.v_ready, 1)
            act.wait_ge(s.small, 7)
            nc.scalar.activation(u2[:, :, 0, :], tmin[:, :, :], ACT.Exp, scale=1.0 - ALPHA).then_inc(s.u_ready, 1)
            nc.scalar.activation(u2[:, :, 1, :], tsum[:, :, :], ACT.Exp, scale=ALPHA - 1.0).then_inc(s.u_ready, 1)

            def unit(h, b, ih):
                act.wait_ge(s.row_in0 if ih == 0 else s.row_in1, 16 * h + 16)
                act.wait_ge(s.bias_ready, h + 1)
                for c in range(NCH):
                    act.wait_ge(s.mask_used, 2 * NCH * h + NCH * ih + c + 1)
                    settle(act)
                    todo = [k for k in range(CJ) if c * CJ + k not in DVE_JT[ih]]
                    for k in todo:
                        step = nc.scalar.activation(mM[:, c, k, :], rows[:, ih, :], ACT.Sigmoid,
                                                    bias=kbias[:, b, c * CJ + k:c * CJ + k + 1], scale=BIG,
                                                    saturate=False)
                    step.then_inc(s.steps, 1)

            with act.Fori(0, H // 2) as hp:
                for b in range(2):
                    for ih in range(2):
                        unit(2 * hp + b, b, ih)

            act.wait_ge(s.dinv_small, 4)
            nc.scalar.activation(dsum[:, :], colsum[:, :], ACT.Sqrt).then_inc(s.dinv_sqrt, 1)
            def pack_hidden(t, k):
                b = k % 2
                act.wait_ge(s.hid_ps, t + 1)
                settle(act)
                nc.scalar.activation(hid[:, b, :].rearrange("p (h c) -> p h c", c=DH),
                                     seq[:, ds(t, 1), :, 0:DH].rearrange("p a h c -> p (a h) c"), ACT.Copy)\
                    .then_inc(s.hid_cp, 1)

            def hidden_T(t, k):
                b = k % 2
                act.wait_ge(s.hid_ps, t + 3)
                act.wait_ge(s.o_ps, t + 1)
                nc.scalar.activation(hT2[:, b, :], ps[:, b, :], ACT.Copy).then_inc(s.hid_T, 1)

            def scaled_relu(t, b):
                act.wait_ge(s.glo, t + 1)
                settle(act)
                nc.scalar.activation(xb[:, b, :], x_slot[:, ds(t, 1), :].rearrange("p a n -> p (a n)"), ACT.Relu,
                                     bias=nmr[:, ds(t, 1)], scale=rstd[:, ds(t, 1)]).then_inc(s.xg_ready, 1)

            def sqrt2(g):
                act.wait_ge(s.ln2_var, g + 1)
                nc.scalar.activation(std[:, :], mv[:, :, 1], ACT.Sqrt).then_inc(s.ln2_std, 1)

            def out_group(g, first=False, last=False):
                for k in range(G):
                    b = k % 2
                    t = G * g + k
                    if not (last and k >= G - 2):
                        pack_hidden(t + 2, k)
                    if not (last and k == G - 1):
                        hidden_T(t + 1, k + 1)
                    act.wait_ge(s.t_ready, t + 3)
                    nc.scalar.activation(nbuf[:, b, :], tbuf[:, b, :], ACT.Exp).then_inc(s.e_ready, 1)
                    if k == 0 and not first:
                        sqrt2(g - 1)
                    if k == 1 and not first:
                        act.wait_ge(s.ln2_ready, g)
                    if not first:
                        for n in NORM_AT[k]:
                            scaled_relu(G * (g - 1) + n, n % 2)

            start_rings(act, s.hid_T, s.z_cp)
            act.wait_ge(s.hidden_ready, 2 * H - 1)
            pack_hidden(0, 0)
            pack_hidden(1, 1)
            hidden_T(0, 0)
            out_group(0, first=True)
            for n in range(4):
                act.wait_ge(s.ne_ps, n + 1)
                nc.scalar.activation(ne_row[:, n * 512:(n + 1) * 512], ps[:, 4 + n, :], ACT.Copy, saturate=False)\
                    .then_inc(s.ne_sb, 1)
            act.wait_ge(s.hidden_ready, 2 * H)
            with act.Fori(1, NG - 1) as g:
                out_group(g)
            out_group(NG - 1, last=True)
            sqrt2(NG - 1)
            act.wait_ge(s.ln2_ready, NG)
            for k in range(G):
                scaled_relu(NT - G + k, k % 2)
            with act.Fori(0, NT // 2) as i:
                for b in range(2):
                    t = 2 * i + b
                    act.wait_ge(s.z_ps, t + 3)
                    act.wait_ge(s.zlo, t + 1)
                    settle(act)
                    nc.scalar.activation(z_tmp[:, b, :], ps[:, b, :], ACT.Copy, scale=dsum[:, ds(t, 1)])\
                        .then_inc(s.z_cp, 1)

        @block.tensor
        def _(pe):
            def transpose_h(t, k):
                pe.wait_ge(s.h_ready, t + 1)
                for c in range(KC):
                    last = nc.tensor.transpose(ps[:, k % 2, c * P:(c + 1) * P], h_buf[:, k % 2, c * P:(c + 1) * P],
                                               ident[:, :])
                last.then_inc(s.hT_ps, 1)

            def tiles(g, last):
                for k in range(G):
                    t = G * g + k
                    b = k % 2
                    if not (last and k == G - 1):
                        transpose_h(t + 1, k + 1)
                    pe.wait_ge(s.hT_sb, t + 1)
                    if k == G - 1:
                        pe.wait_ge(s.wa_red, 2)
                        pe.wait_ge(s.sT_sb, g + 1)
                        settle(pe)
                        for n in range(G):
                            for c in range(KC):
                                mm = nc.tensor.matmul(ps[:, 6, n * 2 * H:(n + 1) * 2 * H],
                                                      hT[:, c, n * P:(n + 1) * P], w12[:, c, :],
                                                      start=(c == 0), stop=(c == KC - 1))
                        mm.then_inc(s.s12_ps, 1)
                    pe.wait_ge(s.seq_sb, t + 1)
                    for c in range(KC):
                        mm = nc.tensor.matmul(ps[:, 2 + b, :], hT[:, c, k * P:(k + 1) * P], wmat[:, c, :],
                                              start=(c == 0), stop=(c == KC - 1))
                    mm.then_inc(s.seq_ps, 1)
                    pe.wait_ge(s.adj_filled, t + 1)
                    for half in range(2):
                        pe.wait_ge((s.at_sb0, s.at_sb1)[half], t + 2)
                        for j in range(NT // 2):
                            jt = half * (NT // 2) + j
                            tr = nc.tensor.transpose(ps_adj[half][:, j, :], adj_b[:, b, jt * P:(jt + 1) * P],
                                                     ident_b[:, :])
                        if half == 0:
                            tr.then_inc(s.at_ps0, 1)
                        if half == 0 and k == G - 1:
                            pe.wait_ge(s.s12_sb, 2 * g + 2)
                            settle(pe)
                            for n in range(G):
                                st = nc.tensor.transpose(ps[0:2 * H, 6, n * P:(n + 1) * P], s_grp[:, n, :],
                                                         ident[:, :])
                            st.then_inc(s.sT_ps, 1)
                    tr.then_inc(s.at_ps1, 1)
                    for j in range(NT):
                        mm = nc.tensor.matmul(ps[:, 7, j:j + 1],
                                              adj_b[:, b, j * P:(j + 1) * P],
                                              ones_b[:, 0:1], start=False, stop=False, skip_group_check=True)
                    mm.then_inc(s.adj_read, 1)

            start_rings(pe, s.hT_ps, s.at_ps1, s.adj_read)
            pe.wait_ge(s.consts, 6)
            nc.tensor.matmul(ps[:, 7, 0:NT], ones_b[:, :], zeros_b[:, :], start=True, stop=False,
                             skip_group_check=True).then_inc(s.col_ps, 1)
            transpose_h(0, 0)
            pe.wait_ge(s.w_in, 16)
            with pe.Fori(0, NG - 1) as g:
                tiles(g, False)
            tiles(NG - 1, True)
            pe.wait_ge(s.small, 2)
            nc.tensor.matmul(ps[:, 6, 0:H], ones_f[:, :], dmax[:, H:2 * H], start=True, stop=True)\
                .then_inc(s.cmax_ps, 1)
            nc.tensor.matmul(ps[:, 6, H:H + NT], ones_p[:, :], empty[:, :], start=True, stop=True)\
                .then_inc(s.ne_cnt, 1)
            pe.wait_ge(s.small, 3)
            pe.wait_ge(s.dinv_small, 2)
            pe.sem_inc(s.mask_used, NCH)
            pe.sem_inc(s.acc_free, 2)

            def unit(h, b, ih):
                u = 2 * h + ih
                pe.wait_ge(s.vals_ready, h + 1)
                pe.wait_ge(s.acc_free, u + 1)
                for c in range(NCH):
                    q = NCH * u + c
                    pe.wait_ge(s.m_ready, q + 1)
                    settle(pe)
                    for k in range(CJ):
                        jt = c * CJ + k
                        for side in range(2):
                            if k == 0 and side == 1:
                                pe.wait_ge(s.n_ready, q + 1)
                                settle(pe)
                            mask = mN if side else mM
                            for t in range(TU):
                                mm = nc.tensor.matmul(
                                    acc[ih][:, t, 0:NPART * 2 * W33].rearrange("p (q s c) -> p q s c", q=NPART, s=2)[:, :, side, :],
                                    mask[:, c, k, t * P:(t + 1) * P], halves[:, b, :, jt, side, :, 1],
                                    start=(jt == 0 and side == 0 and t % 2 == 0),
                                    stop=(jt == NT - 1), skip_group_check=True)
                    mm.then_inc(s.mask_used, 1)

            with pe.Fori(0, H // 2) as hp:
                for b in range(2):
                    for ih in range(2):
                        unit(2 * hp + b, b, ih)

            start_rings(pe, s.hid_ps, s.o_ps, s.z_ps, s.y_ps)
            pe.wait_ge(s.wo_in, 16)
            def transpose_hidden(t, k):
                pe.wait_ge(s.hid_cp, t + 1)
                pe.wait_ge(s.hid_T, t + 1)
                for c in range(KC):
                    tr = nc.tensor.transpose(ps[:, k % 2, c * P:(c + 1) * P], hid[:, k % 2, c * P:(c + 1) * P],
                                             ident[:, :])
                tr.then_inc(s.hid_ps, 1)

            def out_group(g, last):
                for k in range(G):
                    b = k % 2
                    t = G * g + k
                    if not (last and k == G - 1):
                        transpose_hidden(t + 1, k + 1)
                    pe.wait_ge(s.hid_T, t + 3)
                    pe.wait_ge(s.t_ready, t + 1)
                    for c in range(KC):
                        mm = nc.tensor.matmul(ps[:, 2 + b, :], hT2[:, b, c * P:(c + 1) * P], wmat[:, c, :],
                                              start=(c == 0), stop=(c == KC - 1))
                    mm.then_inc(s.o_ps, 1)

            transpose_hidden(0, 0)
            out_group(0, False)
            pe.wait_ge(s.acc_free, 2 * H + 2)
            pe.wait_ge(s.diag_ready, 1)
            for n in range(4):
                nc.tensor.matmul(ps[:, 4 + n, :], ones_b[:, :],
                                 diag.rearrange("p t c -> p (t c)")[:, n * 512:(n + 1) * 512],
                                 start=True, stop=True).then_inc(s.ne_ps, 1)
            with pe.Fori(1, NG - 1) as g:
                out_group(g, False)
            out_group(NG - 1, True)
            def z_products(b, jts, first=False):
                for jt in jts:
                    if first:
                        pe.wait_ge(s.glo, jt + 3)
                    for part in range(2):
                        mm = nc.tensor.matmul(ps[:, b, :], s_buf[:, b, jt, :], g_parts[:, jt, part, :],
                                              start=(jt == 0 and part == 0), stop=(jt == NT - 1 and part == 1))
                return mm

            def z_ready(t):
                pe.wait_ge(s.s_ready, t + 1)
                pe.wait_ge(s.z_cp, t + 1)

            for b in range(2):
                z_ready(b)
                z_products(b, range(NT - G), first=True)
            for b in range(2):
                z_products(b, range(NT - G, NT), first=True).then_inc(s.z_ps, 1)
            with pe.Fori(1, NT // 2) as i:
                for b in range(2):
                    z_ready(2 * i + b)
                    z_products(b, range(NT)).then_inc(s.z_ps, 1)
            with pe.Fori(0, NT // 2) as i:
                for b in range(2):
                    t = 2 * i + b
                    pe.wait_ge(s.a_ready, t + 1)
                    pe.wait_ge(s.y_sb, t + 1)
                    settle(pe)
                    for jt in range(NT):
                        pe.wait_ge(s.zlo, jt + 3)
                        for part in range(2):
                            mm = nc.tensor.matmul(ps[:, 2 + 2 * b + part, :], a_buf[:, b, jt, :],
                                                  z_parts[:, jt, part, :], start=(jt == 0), stop=(jt == NT - 1))
                    mm.then_inc(s.y_ps, 1)

        @block.vector
        def _(dve):
            def norm_stats(g):
                for k in range(G):
                    t = G * g + k
                    st = nc.vector.bn_stats(stats[:, k, :],
                                            x_slot[:, ds(t, 1), :].rearrange("p a n -> p (a n)"))
                st.then_inc(s.st_done, 1)
                dve.wait_ge(s.st_done, g + 1)
                settle(dve)
                for k in range(G):
                    ag = nc.vector.bn_aggr(mv[:, k, :], stats[:, k, :])
                ag.then_inc(s.ag_done, 1)
                dve.wait_ge(s.ag_done, g + 1)
                nc.vector.tensor_scalar(mv[:, :, 1], mv[:, :, 1], EPS, None, ALU.add).then_inc(s.var_ready, 1)

            def norm_scales(g):
                dve.wait_ge(s.std_ready, g + 1)
                settle(dve)
                nc.vector.reciprocal(rstd[:, ds(G * g, G)], std[:, :]).then_inc(s.rs_done, 1)
                dve.wait_ge(s.rs_done, g + 1)
                nc.vector.scalar_tensor_tensor(out=nmr[:, ds(G * g, G)], in0=mv[:, :, 0], scalar=-1.0,
                                               in1=rstd[:, ds(G * g, G)], op0=ALU.mult, op1=ALU.mult)\
                    .then_inc(s.ln_ready, 1)

            def copy_hT(t, k):
                dve.wait_ge(s.hT_ps, t + 3)
                nc.vector.tensor_copy(hT[:, :, (k % G) * P:(k % G + 1) * P],
                                      ps[:, k % 2, :].rearrange("p (c n) -> p c n", c=KC)).then_inc(s.hT_sb, 1)

            def fill_rows(t, b):
                dve.wait_ge(s.adj_cast, t + 1)
                nc.vector.tensor_scalar(empty[:, ds(t, 1)], rowsum[:, ds(t, 1)], 0.0, None, ALU.is_equal)\
                    .then_inc(s.empty_done, 1)
                dve.wait_ge(s.empty_done, t + 1)
                dve.wait_ge(s.adj_read, t + 1)
                nc.vector.tensor_scalar(adj_b[:, b, :], adj_n8[:, ds(t, 1), :].rearrange("p a n -> p (a n)"),
                                        1.0 / ONE8, empty[:, ds(t, 1)], ALU.mult, ALU.max).then_inc(s.adj_filled, 1)

            def sum_wa(n):
                dve.wait_ge(s.wa_mul, n + 1)
                nc.vector.reduce_sum(w12[:, :, n * H:(n + 1) * H], wa_tmp, AX_X).then_inc(s.wa_red, 1)

            def tiles(g, last, first=False):
                for k in range(G):
                    t = G * g + k
                    b = k % 2
                    if first and k < 2:
                        sum_wa(k)
                    if not (last and k == G - 1):
                        if k == G - 1:
                            dve.wait_ge(s.s12_ps, g + 1)
                            dve.wait_ge(s.seq_ps, t)
                            settle(dve)
                        copy_hT(t + 1, k + 1)
                        fill_rows(t + 1, 1 - b)
                    if k == G - 1:
                        dve.wait_ge(s.s12_ps, g + 1)
                        settle(dve)
                        nc.vector.tensor_copy(s_grp[:, :, :], ps[:, 6, 0:G * 2 * H].rearrange("p (t c) -> p t c", t=G))\
                            .then_inc(s.s12_sb, 1)
                        nc.vector.tensor_copy(s12[:, ds(G * g, G), :],
                                              ps[:, 6, 0:G * 2 * H].rearrange("p (t c) -> p t c", t=G))\
                            .then_inc(s.s12_sb, 1)
                        dve.wait_ge(s.sT_ps, g + 1)
                        nc.vector.tensor_copy(st_grp, ps[0:2 * H, 6, :]).then_inc(s.sT_sb, 1)
                        dve.wait_ge(s.sT_sb, g + 2)
                        nc.vector.tensor_scalar(st_rows[:, ds(G * P * g, G * P)].bitcast(U32), st_grp.bitcast(U32),
                                                0xFFFFFFFE, None, ALU.bitwise_and).then_inc(s.rows_sb, 1)
                        nc.vector.reduce_max(gmax[:, ds(g, 1)], st_grp, AX_X).then_inc(s.gmax_done, 1)
                    if k == 0 and not last:
                        norm_stats(g + 1)
                    if k == 1 and not last:
                        norm_scales(g + 1)
                    dve.wait_ge(s.at_ps0, t + 1)
                    nc.vector.tensor_scalar(adj_t8[:, 0:NT // 2, ds(P * t, P)], ps_adj[0], float(ONE8), None, ALU.mult)\
                        .then_inc(s.at_sb0, 1)

            start_rings(dve, s.at_sb0)
            dve.sem_inc(s.sT_sb, 1)
            dve.wait_ge(s.x_first, 16)
            norm_stats(0)
            norm_scales(0)
            copy_hT(0, 0)
            fill_rows(0, 0)
            dve.wait_ge(s.x_second, 16)
            tiles(0, False, first=True)
            dve.wait_ge(s.x_rest, 16 * (NG - 2))
            with dve.Fori(1, NG - 1) as g:
                tiles(g, False)
            tiles(NG - 1, True)

            dve.wait_ge(s.gmax_done, NG)
            nc.vector.reduce_max(smax[:, :], gmax[:, :], AX_X).then_inc(s.small, 1)
            dve.wait_ge(s.s12_sb, 2 * NG)
            nc.vector.tensor_scalar(s2cmp[:, :, :], s12[:, :, H:2 * H], TINY, None, ALU.add).then_inc(s.cmp_ready, 1)
            dve.wait_ge(s.small, 1)
            nc.vector.tensor_scalar(dmax[:, :], ident[0:2 * H, 0:2 * H], smax[:, 0:1], None, ALU.mult)\
                .then_inc(s.small, 1)
            dve.wait_ge(s.cmp_ready, 1)
            nc.vector.tensor_scalar(s2cmp[:, :, :].bitcast(U32), s2cmp[:, :, :].bitcast(U32), 1, None, ALU.bitwise_or)\
                .then_inc(s.cmp_ready, 1)
            dve.wait_ge(s.cmp_ready, 2)
            nc.vector.tensor_scalar(kall[:, :, :], s2cmp[:, :, :], BIG, None, ALU.mult).then_inc(s.all_ready, 1)
            nc.vector.tensor_scalar(nall[:, :, :], s2cmp[:, :, :], -1.0, None, ALU.mult).then_inc(s.all_ready, 1)
            dve.wait_ge(s.cmax_ps, 1)
            dve.wait_ge(s.ne_cnt, 1)
            nc.vector.tensor_copy(cmax[:, :], ps[:, 6, 0:H]).then_inc(s.small, 1)
            dve.wait_ge(s.small, 3)
            c_all = cmax[:, :].unsqueeze(1).broadcast_to([P, NT, H])
            nc.vector.tensor_tensor(tdiff[:, :, :], s12[:, :, H:2 * H], c_all, ALU.subtract).then_inc(s.small, 1)
            nc.vector.tensor_tensor(tsum[:, :, :], s12[:, :, 0:H], c_all, ALU.add).then_inc(s.small, 1)

            def head_scalars(h, b):
                nc.vector.tensor_copy(kbias[:, b, :], kall[:, :, ds(h, 1)].rearrange("p t a -> p (t a)"))
                nc.vector.tensor_copy(negs2[:, b, :], nall[:, :, ds(h, 1)].rearrange("p t a -> p (t a)"))\
                    .then_inc(s.bias_ready, 1)

            def head_values(h, b):
                for side in range(2):
                    last = nc.vector.tensor_tensor(
                        parts[:, b, 0, :, side, :], seq[:, :, ds(h, 1), :].rearrange("p t a c -> p t (a c)"),
                        v2[:, :, side, ds(h, 1)].broadcast_to([P, NT, W33]), ALU.mult)
                last.then_inc(s.prep, 1)

            def head_rest(h, b, part):
                dve.wait_ge(s.prep, 2 * h + part)
                op = nc.vector.tensor_tensor(parts[:, b, part, :, :, :], parts[:, b, part - 1, :, :, :],
                                             halves[:, b, part - 1, :, :, :, 1], ALU.subtract)
                op.then_inc(s.prep if part == 1 else s.vals_ready, 1)

            dve.wait_ge(s.all_ready, 2)
            head_scalars(0, 0)
            dve.wait_ge(s.small, 5)
            nc.vector.tensor_scalar(tmin[:, :, :], tsum[:, :, :], 0.0, None, ALU.min).then_inc(s.small, 1)
            dve.wait_ge(s.small, 6)
            nc.vector.tensor_scalar(tsum[:, :, :], tsum[:, :, :], 0.0, None, ALU.max).then_inc(s.small, 1)
            dve.wait_ge(s.seq_sb, NT + 2)
            dve.wait_ge(s.ones_col, 1)
            dve.wait_ge(s.v_ready, 2)
            head_values(0, 0)
            head_rest(0, 0, 1)
            head_rest(0, 0, 2)
            nc.vector.reduce_sum(n_empty[:, :], ps[:, 6, H:H + NT], AX_X).then_inc(s.dinv_small, 1)
            dve.wait_ge(s.dinv_small, 1)
            dve.wait_ge(s.adj_read, NT + 2)
            nc.vector.tensor_scalar(colsum[:, :], ps[:, 7, 0:NT], n_empty[:, 0:1], None, ALU.subtract)\
                .then_inc(s.dinv_small, 1)
            dve.wait_ge(s.dinv_small, 2)
            nc.vector.scalar_tensor_tensor(out=colsum[:, :], in0=rowsum[:, :], scalar=1.0 / ONE8, in1=colsum[:, :],
                                           op0=ALU.mult, op1=ALU.add).then_inc(s.dinv_small, 1)
            dve.wait_ge(s.dinv_small, 3)
            nc.vector.tensor_scalar(colsum[:, :], colsum[:, :], 0.5, 1.0, ALU.mult, ALU.add).then_inc(s.dinv_small, 1)

            def unit(h, b, ih, u, first, last):
                def step(c):
                    if any(c * CJ <= j < (c + 1) * CJ for j in DVE_JT[ih]):
                        dve.wait_ge(s.mask_used, NCH * u + c + 1)
                        settle(dve)
                    for j in DVE_JT[ih]:
                        if c * CJ <= j < (c + 1) * CJ:
                            nc.vector.tensor_scalar(mM[:, c, j - c * CJ, :], rows[:, ih, :], negs2[:, b, j:j + 1], None,
                                                    ALU.is_gt, saturate=False).then_inc(s.m_dve, 1)

                dve.wait_ge(s.row_in0 if ih == 0 else s.row_in1, 16 * h + 16)
                step(0)
                before = (u - ih) // 2 * DVE_PER_HEAD if isinstance(u, int) else h * DVE_PER_HEAD
                before = before + len(DVE_JT[0]) * ih
                for c in range(NCH):
                    q = NCH * u + c
                    adj_c = adj_t[:, c * CJ:(c + 1) * CJ, ih * HALF:(ih + 1) * HALF].bitcast(U32)
                    done = sum(j < (c + 1) * CJ for j in DVE_JT[ih])
                    if not (isinstance(before, int) and before + done == 0):
                        dve.wait_ge(s.m_dve, before + done)
                    dve.wait_ge(s.steps, q + 1)
                    nc.vector.tensor_tensor(mM[:, c, :, :].bitcast(U32), mM[:, c, :, :].bitcast(U32), adj_c,
                                            ALU.bitwise_and).then_inc(s.m_ready, 1)
                    if c < NCH - 1:
                        step(c + 1)
                    dve.wait_ge(s.m_ready, q + 1)
                    nc.vector.tensor_tensor(mN[:, c, :, :].bitcast(U32), mM[:, c, :, :].bitcast(U32), adj_c,
                                            ALU.bitwise_xor).then_inc(s.n_ready, 1)
                    if ih == 0 and c == 1 and not last:
                        dve.wait_ge(s.mask_used, NCH * (u + 1))
                        dve.wait_ge(s.vals_ready, h + 1)
                        settle(dve)
                        head_values(h + 1, 1 - b)
                    if ih == 0 and c == 2 and not last:
                        head_rest(h + 1, 1 - b, 1)
                    if ih == 0 and c == 3 and not last:
                        head_rest(h + 1, 1 - b, 2)
                    if ih == 1 and c == 0 and not last:
                        head_scalars(h + 1, 1 - b)
                    if c == 0 and not (first and b == 0):
                        divide_unit(u - 2, ih)
                if not (first and b == 0 and ih == 0):
                    reduce_unit(u - 1, 1 - ih)

            def reduce_unit(u, ih):
                dve.wait_ge(s.mask_used, NCH * (u + 2))
                if not isinstance(u, int) or u > 0:
                    dve.wait_ge(s.hidden_ready, u)
                nc.vector.reduce_sum(red[:, ih, :, :, :].rearrange("p t s c -> p t (s c)"),
                                     acc[ih][:, :, 0:NPART * 2 * W33].rearrange("p t (q c) -> p t c q", q=NPART),
                                     AX_X).then_inc(s.acc_free, 1)

            def divide_unit(u, ih):
                dve.wait_ge(s.summed, u + 1)
                nc.vector.reciprocal(rden[:, ih, :], fin[:, :, DH]).then_inc(s.recip, 1)

            def pair_of_heads(hp, first=False, last=False):
                for b in range(2):
                    for ih in range(2):
                        unit(2 * hp + b, b, ih, 4 * hp + 2 * b + ih, first, last and b == 1)

            pair_of_heads(0, first=True)
            with dve.Fori(1, H // 2 - 1) as hp:
                pair_of_heads(hp)
            pair_of_heads(H // 2 - 1, last=True)
            U = 2 * H
            divide_unit(U - 2, 0)
            dve.wait_ge(s.mask_used, NCH * (U + 1))
            nc.vector.tensor_scalar(empty[:, :], empty[:, :], -1.0, 1.0, ALU.mult, ALU.add).then_inc(s.empty_done, 1)
            reduce_unit(U - 1, 1)
            divide_unit(U - 1, 1)
            dve.wait_ge(s.empty_done, NT + 1)
            nc.vector.tensor_tensor(diag, ident_b[:, :].unsqueeze(1).broadcast_to([P, NT, P]),
                                    empty[:, :].unsqueeze(2).broadcast_to([P, NT, P]), ALU.mult)\
                .then_inc(s.diag_ready, 1)

            dve.wait_ge(s.dinv_sqrt, 1)
            nc.vector.reciprocal(dinv[:, :], dsum[:, :]).then_inc(s.dinv_ready, 1)
            dve.wait_ge(s.dinv_ready, 1)
            nc.vector.tensor_scalar(dsum[:, :], dinv[:, :], 0.5 * Z_SCALE * LO_SCALE / (G_SCALE * ONE8), None, ALU.mult)\
                .then_inc(s.dinv_ready, 1)

            def tile_of(buf, t):
                return buf[:, ds(t, 1), :].rearrange("p a n -> p (a n)")

            def norm2_scales(g):
                dve.wait_ge(s.ln2_std, g + 1)
                settle(dve)
                nc.vector.reciprocal(rstd[:, ds(G * g, G)], std[:, :]).then_inc(s.ln2_small, 1)
                dve.wait_ge(s.ln2_small, 2 * g + 1)
                nc.vector.scalar_tensor_tensor(out=rstd[:, ds(G * g, G)], in0=rstd[:, ds(G * g, G)], scalar=G_SCALE,
                                               in1=dinv[:, ds(G * g, G)], op0=ALU.mult, op1=ALU.mult)\
                    .then_inc(s.ln2_small, 1)
                dve.wait_ge(s.ln2_small, 2 * g + 2)
                nc.vector.scalar_tensor_tensor(out=nmr[:, ds(G * g, G)], in0=mv[:, :, 0], scalar=-1.0,
                                               in1=rstd[:, ds(G * g, G)], op0=ALU.mult, op1=ALU.mult)\
                    .then_inc(s.ln2_ready, 1)

            def high_part(t, b):
                dve.wait_ge(s.xg_ready, t + 1)
                nc.vector.tensor_copy(g_parts[:, ds(t, 1), 0, :].rearrange("p a n -> p (a n)"), xb[:, b, :])\
                    .then_inc(s.ghi, 1)

            ne_cols = ne_row.bitcast(U32)

            def true_columns(buf, t):
                return nc.vector.tensor_tensor(
                    buf, adj_t[:, :, :].bitcast(U32)[:, :, ds(P // 4 * t, P // 4)],
                    ne_cols[:, ds(P // 4 * t, P // 4)].unsqueeze(1).broadcast_to([P, NT, P // 4]), ALU.bitwise_and)

            def build_s(t, b):
                true_columns(col_buf.bitcast(U32), t).then_inc(s.col_true, 1)
                dve.wait_ge(s.col_true, t + 1)
                dve.wait_ge(s.z_ps, t + 1)
                nc.vector.tensor_tensor(s_buf[:, b, :, :], col_buf.bitcast(U8), adj_n8[:, :, ds(P * t, P)],
                                        ALU.add).then_inc(s.s_sum, 1)
                dve.wait_ge(s.s_sum, t + 1)
                nc.vector.scalar_tensor_tensor(out=tile_of(s_buf[:, b], t), in0=ident_b[:, :], scalar=2.0 * ONE8,
                                               in1=tile_of(s_buf[:, b], t), op0=ALU.mult, op1=ALU.add)\
                    .then_inc(s.s_ready, 1)

            def stats2(t, k):
                dve.wait_ge(s.x1_ready, t + 1)
                settle(dve)
                nc.vector.bn_stats(stats[:, k, :], tile_of(x_slot, t)).then_inc(s.ln2_st, 1)
                dve.wait_ge(s.ln2_st, t + 1)
                settle(dve)
                nc.vector.bn_aggr(mv[:, k, :], stats[:, k, :]).then_inc(s.ln2_ag, 1)

            def var2(g):
                dve.wait_ge(s.ln2_ag, G * g + G)
                nc.vector.tensor_scalar(mv[:, :, 1], mv[:, :, 1], EPS, None, ALU.add).then_inc(s.ln2_var, 1)

            def out_group(g, first=False, last=False):
                for k in range(G):
                    b = k % 2
                    t = G * g + k
                    dve.wait_ge(s.o_ps, t + 3)
                    nc.vector.tensor_tensor(tbuf[:, b, :], ps[:, 2 + b, :], b_row[:, :], ALU.add).then_inc(s.t_ready, 1)
                    if k == 1 and not first:
                        norm2_scales(g - 1)
                    if not (first and k == 0):
                        stats2(t - 1, (k - 1) % G)
                    if k == 0 and not first:
                        var2(g - 1)
                    dve.wait_ge(s.e_ready, t + 1)
                    nc.vector.tensor_scalar(nbuf[:, b, :], nbuf[:, b, :], 1.0, -1.0, ALU.min, ALU.add)\
                        .then_inc(s.em_ready, 1)
                    dve.wait_ge(s.em_ready, t + 1)
                    nc.vector.scalar_tensor_tensor(out=nbuf[:, b, :], in0=tbuf[:, b, :], scalar=0.0, in1=nbuf[:, b, :],
                                                   op0=ALU.max, op1=ALU.add).then_inc(s.q_ready, 1)
                    if not first:
                        for n in NORM_AT[k]:
                            high_part(G * (g - 1) + n, n % 2)
                    if last and k in (1, 2):
                        build_s(k - 1, k - 1)

            start_rings(dve, s.t_ready)
            dve.wait_ge(s.b_in, 16)
            out_group(0, first=True)
            with dve.Fori(1, NG - 1) as g:
                out_group(g)
            dve.wait_ge(s.ne_sb, 4)
            out_group(NG - 1, last=True)
            stats2(NT - 1, G - 1)
            var2(NG - 1)
            norm2_scales(NG - 1)
            dve.wait_ge(s.glo, NT - G + 2)
            for k in range(G):
                t = NT - G + k
                high_part(t, k % 2)
                dve.wait_ge(s.ghi, t + 1)
                nc.vector.tensor_tensor(g_parts[:, t, 1, :], xb[:, k % 2, :], g_parts[:, t, 0, :], ALU.subtract)\
                    .then_inc(s.glo, 1)

            def copy_a(t, b):
                dve.wait_ge(s.y_ps, t + 1)
                true_columns(a_buf[:, b, :, :].bitcast(U32), t).then_inc(s.a_ready, 1)

            def split_z(t, b):
                dve.wait_ge(s.z_cp, t + 3)
                nc.vector.tensor_scalar(z_parts[:, ds(t, 1), 0, :].rearrange("p a n -> p (a n)"), z_tmp[:, b, :],
                                        1.0 / LO_SCALE, None, ALU.mult).then_inc(s.zhi, 1)
                dve.wait_ge(s.zhi, t + 1)
                nc.vector.scalar_tensor_tensor(out=z_parts[:, ds(t, 1), 1, :].rearrange("p a n -> p (a n)"),
                                               in0=z_parts[:, ds(t, 1), 0, :].rearrange("p a n -> p (a n)"),
                                               scalar=-LO_SCALE, in1=z_tmp[:, b, :], op0=ALU.mult, op1=ALU.add)\
                    .then_inc(s.zlo, 1)

            start_rings(dve, s.zlo, s.y_sb)
            with dve.Fori(0, NT // 2 - 1) as i:
                for b in range(2):
                    split_z(2 * i + b, b)
                    build_s(2 * i + b + 2, b)
            split_z(NT - 2, 0)
            dve.wait_ge(s.z_ps, NT + 1)
            copy_a(0, 0)
            split_z(NT - 1, 1)
            def finish_y(t, b, i):
                dve.wait_ge(s.y_ps, t + 3)
                dve.wait_ge((s.out_done0, s.out_done1)[b], 16 * i + 16)
                nc.vector.scalar_tensor_tensor(out=o_tmp[:, b, :], in0=ps[:, 2 + 2 * b, :], scalar=1.0 / Z_SCALE,
                                               in1=tile_of(x_slot, t), op0=ALU.mult, op1=ALU.add)\
                    .then_inc(s.y_hi, 1)
                dve.wait_ge(s.y_hi, t + 1)
                nc.vector.scalar_tensor_tensor(out=o_tmp[:, b, :], in0=ps[:, 3 + 2 * b, :],
                                               scalar=1.0 / (Z_SCALE * LO_SCALE), in1=o_tmp[:, b, :],
                                               op0=ALU.mult, op1=ALU.add).then_inc(s.y_sb, 1)

            with dve.Fori(0, NT // 2 - 1) as i:
                for b in range(2):
                    copy_a(2 * i + b + 1, 1 - b)
                    finish_y(2 * i + b, b, i)
            copy_a(NT - 1, 1)
            finish_y(NT - 2, 0, NT // 2 - 1)
            finish_y(NT - 1, 1, NT // 2 - 1)


_INS = ["x", "adj", "L0_gnn_W_seq", "L0_gnn_a1", "L0_gnn_a2", "L0_gnn_W_out", "L0_gnn_b_out"]


def kernel(**inputs):
    import numpy as np
    import concourse.bacc as bacc
    from concourse.bass_utils import run_bass_kernel_spmd

    nc = bacc.Bacc("TRN2", target_bir_lowering=False, num_devices=1)
    arrays, args = {}, []
    for name in _INS:
        a = np.ascontiguousarray(inputs[name])
        arrays[f"in_{name}"] = a
        args.append(nc.dram_tensor(f"in_{name}", a.shape, mybir.dt.from_np(a.dtype), kind="ExternalInput").ap())
    out = nc.dram_tensor("out", inputs["x"].shape, F32, kind="ExternalOutput").ap()
    gat_gcn(nc, *args, out)
    r = run_bass_kernel_spmd(nc, [arrays], core_ids=[0])
    return r.results[0]["out"]
```

```python
from contextlib import ExitStack

import concourse.bass as bass
from concourse import mybir

P = 128
F32 = mybir.dt.float32
BF16 = mybir.dt.bfloat16
F16 = mybir.dt.float16
FP8 = mybir.dt.float8e4
U32 = mybir.dt.uint32
U8 = mybir.dt.uint8
ALU = mybir.AluOpType
ACT = mybir.ActivationFunctionType
AX_X = mybir.AxisListType.X
ds = bass.ds


class Semaphores:

    def __init__(self, sem):
        self.settled = sem("settled")
        self.w_in = sem("w_in")
        self.a_in = sem("a_in")
        self.x_first = sem("x_first")
        self.x_second = sem("x_second")
        self.x_rest = sem("x_rest")
        self.adj_in0 = sem("adj_in0")
        self.adj_in1 = sem("adj_in1")
        self.consts0 = sem("consts0")
        self.consts = sem("consts")
        self.wa_mul = sem("wa_mul")
        self.wa_red = sem("wa_red")
        self.st_done = sem("st_done")
        self.ag_done = sem("ag_done")
        self.var_ready = sem("var_ready")
        self.std_ready = sem("std_ready")
        self.rs_done = sem("rs_done")
        self.ln_ready = sem("ln_ready")
        self.h_ready = sem("h_ready")
        self.hT_ps = sem("hT_ps")
        self.hT_sb = sem("hT_sb")
        self.seq_ps = sem("seq_ps")
        self.seq_sb = sem("seq_sb")
        self.ones_col = sem("ones_col")
        self.adj_cast = sem("adj_cast")
        self.empty_done = sem("empty_done")
        self.adj_filled = sem("adj_filled")
        self.at_ps0 = sem("at_ps0")
        self.at_ps1 = sem("at_ps1")
        self.at_sb0 = sem("at_sb0")
        self.at_sb1 = sem("at_sb1")
        self.adj_read = sem("adj_read")
        self.sT_ps = sem("sT_ps")
        self.sT_sb = sem("sT_sb")
        self.gmax_done = sem("gmax_done")
        self.s12_ps = sem("s12_ps")
        self.s12_sb = sem("s12_sb")
        self.rows_sb = sem("rows_sb")
        self.rows_out = sem("rows_out")
        self.small = sem("small")
        self.cmax_ps = sem("cmax_ps")
        self.ne_cnt = sem("ne_cnt")
        self.v_ready = sem("v_ready")
        self.u_ready = sem("u_ready")
        self.cmp_ready = sem("cmp_ready")
        self.all_ready = sem("all_ready")
        self.row_in0 = sem("row_in0")
        self.row_in1 = sem("row_in1")
        self.bias_ready = sem("bias_ready")
        self.steps = sem("steps")
        self.m_dve = sem("m_dve")
        self.m_ready = sem("m_ready")
        self.n_ready = sem("n_ready")
        self.mask_used = sem("mask_used")
        self.acc_free = sem("acc_free")
        self.sums_half = sem("sums_half")
        self.prep = sem("prep")
        self.vals_ready = sem("vals_ready")
        self.weighed = sem("weighed")
        self.summed = sem("summed")
        self.recip = sem("recip")
        self.hidden_ready = sem("hidden_ready")
        self.dinv_small = sem("dinv_small")
        self.dinv_sqrt = sem("dinv_sqrt")
        self.dinv_ready = sem("dinv_ready")
        self.wo_in = sem("wo_in")
        self.b_in = sem("b_in")
        self.xr_in0 = sem("xr_in0")
        self.xr_in1 = sem("xr_in1")
        self.diag_ready = sem("diag_ready")
        self.ne_ps = sem("ne_ps")
        self.ne_sb = sem("ne_sb")
        self.hid_cp = sem("hid_cp")
        self.hid_ps = sem("hid_ps")
        self.hid_T = sem("hid_T")
        self.o_ps = sem("o_ps")
        self.t_ready = sem("t_ready")
        self.e_ready = sem("e_ready")
        self.em_ready = sem("em_ready")
        self.q_ready = sem("q_ready")
        self.x1_ready = sem("x1_ready")
        self.ln2_st = sem("ln2_st")
        self.ln2_ag = sem("ln2_ag")
        self.ln2_var = sem("ln2_var")
        self.ln2_std = sem("ln2_std")
        self.ln2_small = sem("ln2_small")
        self.ln2_ready = sem("ln2_ready")
        self.xg_ready = sem("xg_ready")
        self.ghi = sem("ghi")
        self.glo = sem("glo")
        self.col_true = sem("col_true")
        self.s_sum = sem("s_sum")
        self.s_ready = sem("s_ready")
        self.z_ps = sem("z_ps")
        self.z_cp = sem("z_cp")
        self.zhi = sem("zhi")
        self.zlo = sem("zlo")
        self.a_ready = sem("a_ready")
        self.y_ps = sem("y_ps")
        self.y_hi = sem("y_hi")
        self.y_sb = sem("y_sb")
        self.out_done0 = sem("out_done0")
        self.out_done1 = sem("out_done1")


def gat_gcn(nc, x, adj, w_seq, a1, a2, w_out, b_out, out):
    N, D = x.shape
    DH = a1.shape[0]
    H = D // DH
    NT = N // P
    KC = D // P
    G = 4
    NG = NT // G
    TU = NT // 2
    CJ = 2
    NCH = NT // CJ
    NSLOT = 4
    NPART = 3
    W33 = DH + 1
    SLOT = H * W33
    ALPHA = 0.2
    EPS = 1e-5
    BIG = 2.0 ** 90
    TINY = 2.0 ** -50
    G_SCALE = 2.0 ** 10
    Z_SCALE = 2.0 ** 5
    LO_SCALE = 2.0 ** 11
    ONE8 = 0x38
    MINUS8 = 0xB8
    DVE_JT = (1, 7, 13)
    REDUCE_AT = (0, 0)
    DIVIDE_AT = (1, 2)
    XOR_CH = (1, 2, 4, 5, 6)
    NORM_AT = ((), (0,), (1,), (2, 3))

    s1_dram = nc.dram_tensor("s1_rows", [H, N], F32, kind="Internal").ap()

    with ExitStack() as ctx:
        def sb(name, shape, dt):
            return ctx.enter_context(nc.sbuf_tensor(name, shape, dt))

        def sem(name):
            return ctx.enter_context(nc.semaphore(name))

        adj_t = sb("adj_t", [P, NT, N], FP8)
        adj_n = sb("adj_n", [P, NT, N], FP8)
        nodes = sb("nodes", [P, NT, SLOT], F32)
        wmat = sb("wmat", [P, KC, D], F32)
        masks = sb("masks", [P, 32768], FP8)
        small_bufs = sb("small_bufs", [P, 3 * N], BF16)
        rows = sb("rows", [P, N], F32)
        work = sb("work", [P, 8192], F32)

        ident = sb("ident", [P, P], F32)
        ident_b = sb("ident_b", [P, P], BF16)
        ones_b = sb("ones_b", [P, P], BF16)
        zeros_b = sb("zeros_b", [P, NT], BF16)
        ones_p = sb("ones_p", [P, P], F32)
        ones_f = sb("ones_f", [2 * H, P], F32)
        a12 = sb("a12", [P, 2, DH], F32)
        w12 = sb("w12", [P, KC, 2 * H], F32)
        stats = sb("stats", [P, G, 6], F32)
        mv = sb("mv", [P, G, 2], F32)
        std = sb("std", [P, G], F32)
        rstd = sb("rstd", [P, NT], F32)
        nmr = sb("nmr", [P, NT], F32)
        rowsum = sb("rowsum", [P, NT], F32)
        empty = sb("empty", [P, NT], F32)
        colsum = sb("colsum", [P, NT], F32)
        dinv = sb("dinv", [P, NT], F32)
        dsum = sb("dsum", [P, NT], F32)
        b_row = sb("b_row", [P, D], F32)
        s_grp = sb("s_grp", [P, G, 2 * H], F32)
        s12 = sb("s12", [P, NT, 2 * H], F32)
        gmax = sb("gmax", [2 * H, NG], F32)
        smax = sb("smax", [2 * H, 1], F32)
        dmax = sb("dmax", [2 * H, 2 * H], F32)
        cmax = sb("cmax", [P, H], F32)
        tdiff = sb("tdiff", [P, NT, H], F32)
        tsum = sb("tsum", [P, NT, H], F32)
        tmin = sb("tmin", [P, NT, H], F32)
        v2 = sb("v2", [P, NT, 2, H], F32)
        u2 = sb("u2", [P, NT, 2, H], F32)
        n_empty = sb("n_empty", [P, 1], F32)
        kall = sb("kall", [P, NT, H], F32)
        nall = sb("nall", [P, NT, H], F32)
        s2cmp = sb("s2cmp", [P, NT, H], F32)
        kbias = sb("kbias", [P, 2, NT], F32)
        negs2 = sb("negs2", [P, 2, NT], F32)
        rden = sb("rden", [P, 2, TU], F32)

        x_slot = nodes[:, :, 0:D]
        seq = nodes[:, :, :].rearrange("p t (h c) -> p t h c", c=W33)
        stage = masks[:, :].bitcast(F32)
        adj_in = stage[:, 0:2 * N].rearrange("p (b n) -> p b n", b=2)
        adj_b = stage[:, 2 * N:3 * N].bitcast(BF16).rearrange("p (b n) -> p b n", b=2)
        h_buf = stage[:, 3 * N:3 * N + 2 * D].rearrange("p (b n) -> p b n", b=2)
        adj_t8 = adj_t[:, :, :].bitcast(U8)
        adj_n8 = adj_n[:, :, :].bitcast(U8)
        mM = masks[:, 0:16384].rearrange("p (c j i) -> p c j i", c=NSLOT, j=CJ)
        mN = masks[:, 16384:32768].rearrange("p (c j i) -> p c j i", c=NSLOT, j=CJ)
        g_parts = masks[:, :].bitcast(F16).rearrange("p (t s n) -> p t s n", s=2, n=D)
        wa_tmp = small_bufs[:, 0:2 * KC * D].bitcast(F32).rearrange("p (k h d) -> p k h d", k=KC, d=DH)
        s_buf = small_bufs[:, 0:2 * N].rearrange("p (b t i) -> p b t i", b=2, t=NT)
        a_buf = small_bufs[:, 0:N].bitcast(FP8).rearrange("p (b t i) -> p b t i", b=2, t=NT)
        z_tmp = small_bufs[:, 2 * N:2 * N + 4 * D].bitcast(F32).rearrange("p (b n) -> p b n", b=2)
        o_tmp = small_bufs[:, N:N + 4 * D].bitcast(F32).rearrange("p (b n) -> p b n", b=2)
        st_grp = b_row[0:2 * H, 0:G * P]
        st_rows = rows[0:2 * H, :]
        head_row = (rows[:, :], small_bufs[:, 0:2 * N].bitcast(F32))
        hT = work[:, 0:KC * G * P].rearrange("p (k n) -> p k n", k=KC)
        VALS = NPART * NT * 2 * W33
        parts = work[:, 0:2 * VALS].rearrange("p (b q t s c) -> p b q t s c", b=2, q=NPART, t=NT, s=2)
        halves = work[:, 0:2 * VALS].bitcast(BF16).rearrange("p (b q t s c w) -> p b q t s c w", b=2, q=NPART, t=NT,
                                                             s=2, w=2)
        rest = work[:, 2 * VALS:]
        red = rest[:, 0:2 * TU * 2 * W33].rearrange("p (b t s c) -> p b t s c", b=2, t=TU, s=2)
        fin = rest[:, 2 * TU * 2 * W33:3 * TU * 2 * W33].rearrange("p (t s c) -> p t s c", t=TU, s=2)[:, :, 0, :]

        def pair(n):
            return work[:, 2 * D * n:2 * D * n + 2 * D].rearrange("p (b n) -> p b n", b=2)
        hid, hT2, tbuf, nbuf, xr, xb = (pair(n) for n in range(6))
        ne_row = rows[:, 0:N // 4].bitcast(FP8)
        col_buf = rows[:, N // 4:N // 2].rearrange("p (t i) -> p t i", t=NT)
        z_parts = work[:, :].bitcast(F16).rearrange("p (t s n) -> p t s n", s=2, n=D)
        diag = small_bufs[:, 2 * N:3 * N].rearrange("p (t c) -> p t c", t=NT)

        ps = ctx.enter_context(nc.psum_tensor("ps", [P, 8, 512], F32))
        ps_adj = [ps[:, 4 + b, :].bitcast(BF16).rearrange("p (t i) -> p t i", i=P) for b in range(2)]
        acc = ps[:, :, :].rearrange("p b (t c) -> p (b t) c", t=2)[:, :, 0:NPART * 2 * W33]

        s = Semaphores(sem)

        def x_loads(t, b):
            return 8 * (t - b) + 16

        def settle(eng):
            eng.sem_inc(s.settled, 1)

        def start_rings(eng, *names):
            for name in names:
                eng.sem_inc(name, 2)

        block = ctx.enter_context(nc.Block())

        @block.sync
        def _(sp):
            x_t = x.rearrange("(g t p) n -> g p t n", t=G, p=P)
            adj_tiles = adj.rearrange("(t p) n -> t p n", p=P)
            sp.dma_start(x_slot[:, 0:G, :], x_t[0]).then_inc(s.x_first, 16)
            sp.dma_start(wmat[:, :, :], w_seq.rearrange("(k p) n -> p k n", p=P)).then_inc(s.w_in, 16)
            sp.dma_start(a12[:, 0, :], a1.rearrange("(a d) -> a d", a=1).partition_broadcast(P)).then_inc(s.a_in, 16)
            sp.dma_start(a12[:, 1, :], a2.rearrange("(a d) -> a d", a=1).partition_broadcast(P)).then_inc(s.a_in, 16)
            sp.dma_start(adj_in[:, 0, :], adj_tiles[0]).then_inc(s.adj_in0, 16)
            sp.dma_start(adj_in[:, 1, :], adj_tiles[1]).then_inc(s.adj_in1, 16)
            sp.dma_start(x_slot[:, G:2 * G, :], x_t[1]).then_inc(s.x_second, 16)

            def adj_pair(i):
                sp.wait_ge(s.adj_cast, 2 * i + 1)
                sp.dma_start(adj_in[:, 0, :], adj_tiles[ds(2 * i + 2, 1)].rearrange("a p n -> (a p) n"))\
                    .then_inc(s.adj_in0, 16)
                sp.wait_ge(s.adj_cast, 2 * i + 2)
                sp.dma_start(adj_in[:, 1, :], adj_tiles[ds(2 * i + 3, 1)].rearrange("a p n -> (a p) n"))\
                    .then_inc(s.adj_in1, 16)

            adj_pair(0)
            for g in range(2, NG):
                sp.dma_start(x_slot[:, g * G:(g + 1) * G, :], x_t[g]).then_inc(s.x_rest, 16)
            with sp.Fori(1, NT // 2 - 1) as i:
                adj_pair(i)
            row_in = (s.row_in0, s.row_in1)
            most = (NG - 1) * G * P
            for n, part in enumerate((slice(0, most), slice(most, N))):
                sp.wait_ge(s.rows_sb, NG - 1 + n)
                sp.dma_start(s1_dram[:, part], st_rows[0:H, part]).then_inc(s.rows_out, 16)
                sp.wait_ge(s.rows_out, 16 * n + 16)
                for b in range(2):
                    sp.dma_start(head_row[b][:, part], s1_dram[b:b + 1, part].partition_broadcast(P))\
                        .then_inc(row_in[b], 16)
            sp.wait_ge(s.seq_ps, NT)
            sp.dma_start(wmat[:, :, :], w_out.rearrange("(k p) n -> p k n", p=P)).then_inc(s.wo_in, 16)
            with sp.Fori(0, H // 2 - 1) as hp:
                for b in range(2):
                    sp.wait_ge(s.steps, NCH * (2 * hp + b + 1))
                    sp.wait_ge(s.m_ready, NCH * (2 * hp + b + 1))
                    sp.dma_start(head_row[b], s1_dram[ds(2 * hp + b + 2, 1), :].partition_broadcast(P))\
                        .then_inc(row_in[b], 16)
            sp.wait_ge(s.mask_used, NCH * H + NSLOT)
            sp.dma_start(b_row[:, :], b_out.rearrange("(a d) -> a d", a=1).partition_broadcast(P)).then_inc(s.b_in, 16)
            x_tiles = x.rearrange("(t p) n -> t p n", p=P)
            sp.dma_start(xr[:, 0, :], x_tiles[0]).then_inc(s.xr_in0, 16)
            sp.dma_start(xr[:, 1, :], x_tiles[1]).then_inc(s.xr_in1, 16)
            with sp.Fori(0, NT // 2 - 1) as i:
                sp.wait_ge(s.x1_ready, 2 * i + 1)
                sp.dma_start(xr[:, 0, :], x_tiles[ds(2 * i + 2, 1)].rearrange("a p n -> (a p) n"))\
                    .then_inc(s.xr_in0, 16)
                sp.wait_ge(s.x1_ready, 2 * i + 2)
                sp.dma_start(xr[:, 1, :], x_tiles[ds(2 * i + 3, 1)].rearrange("a p n -> (a p) n"))\
                    .then_inc(s.xr_in1, 16)
            sp.sem_inc(s.out_done0, 16)
            sp.sem_inc(s.out_done1, 16)
            out_tiles = out.rearrange("(t p) n -> t p n", p=P)
            with sp.Fori(0, NT // 2) as i:
                for b in range(2):
                    sp.wait_ge(s.y_sb, 2 * i + b + 3)
                    sp.dma_start(out_tiles[ds(2 * i + b, 1)].rearrange("a p n -> (a p) n"), o_tmp[:, b, :])\
                        .then_inc((s.out_done0, s.out_done1)[b], 16)
            sp.wait_ge(s.out_done0, 8 * NT + 16)
            sp.wait_ge(s.out_done1, 8 * NT + 16)

        @block.gpsimd
        def _(pool):
            nc.gpsimd.memset(ident[:, :], 0.0).then_inc(s.consts0, 1)
            nc.gpsimd.memset(ones_b[:, :], 1.0).then_inc(s.consts, 1)
            nc.gpsimd.memset(ones_f[:, :], 1.0).then_inc(s.consts, 1)
            nc.gpsimd.memset(ones_p[:, :], 1.0).then_inc(s.consts, 1)
            nc.gpsimd.memset(zeros_b[:, :], 0.0).then_inc(s.consts, 1)
            pool.wait_ge(s.consts0, 1)
            nc.gpsimd.affine_select(out=ident[:, :], in_=ident[:, :], compare_op=ALU.not_equal, fill=1.0, base=0,
                                    pattern=[[-1, P]], channel_multiplier=1).then_inc(s.consts, 1)
            pool.wait_ge(s.consts, 5)
            nc.gpsimd.tensor_copy(ident_b[:, :], ident[:, :]).then_inc(s.consts, 1)
            pool.wait_ge(s.w_in, 16)
            pool.wait_ge(s.a_in, 32)
            for n in range(2):
                if n:
                    pool.wait_ge(s.wa_red, n)
                nc.gpsimd.tensor_tensor(wa_tmp, wmat[:, :, :].rearrange("p k (h d) -> p k h d", d=DH),
                                        a12[:, n, :].unsqueeze(1).unsqueeze(1).broadcast_to([P, KC, H, DH]),
                                        ALU.mult).then_inc(s.wa_mul, 1)
            pool.wait_ge(s.h_ready, NT)
            nc.gpsimd.memset(seq[:, :, :, DH:W33], 1.0).then_inc(s.ones_col, 1)

            def finish_half(h, half):
                n = 2 * h + half
                t0 = half * TU
                pool.wait_ge(s.acc_free, n + 3)
                settle(pool)
                nc.gpsimd.tensor_tensor(
                    red[:, half, :, :, :], red[:, half, :, :, :],
                    u2[:, t0:t0 + TU, :, ds(h, 1)].broadcast_to([P, TU, 2, W33]), ALU.mult).then_inc(s.weighed, 1)
                pool.wait_ge(s.weighed, n + 1)
                nc.gpsimd.tensor_tensor(fin, red[:, half, :, 0, :], red[:, half, :, 1, :], ALU.subtract)\
                    .then_inc(s.summed, 1)
                pool.wait_ge(s.recip, n + 1)
                settle(pool)
                nc.gpsimd.tensor_tensor(
                    seq[:, t0:t0 + TU, ds(h, 1), 0:DH].rearrange("p t a c -> p t (a c)"), fin[:, :, 0:DH],
                    rden[:, half, :].unsqueeze(2).broadcast_to([P, TU, DH]), ALU.mult).then_inc(s.hidden_ready, 1)

            pool.wait_ge(s.u_ready, 2)
            with pool.Fori(0, H) as h:
                for half in range(2):
                    finish_half(h, half)

            start_rings(pool, s.glo)

            def add_x(t, b):
                pool.wait_ge(s.q_ready, t + 1)
                pool.wait_ge(s.xr_in0 if b == 0 else s.xr_in1, x_loads(t, b))
                settle(pool)
                nc.gpsimd.tensor_tensor(x_slot[:, ds(t, 1), :].rearrange("p a n -> p (a n)"), nbuf[:, b, :],
                                        xr[:, b, :], ALU.add).then_inc(s.x1_ready, 1)

            def low_part(t, b):
                pool.wait_ge(s.ghi, t + 1)
                settle(pool)
                nc.gpsimd.tensor_tensor(g_parts[:, ds(t, 1), 1, :].rearrange("p a n -> p (a n)"), xb[:, b, :],
                                        g_parts[:, ds(t, 1), 0, :].rearrange("p a n -> p (a n)"), ALU.subtract)\
                    .then_inc(s.glo, 1)

            for k in range(G):
                add_x(k, k % 2)
            with pool.Fori(1, NG) as g:
                for k in range(G):
                    add_x(G * g + k, k % 2)
                    for n in NORM_AT[k]:
                        low_part(G * (g - 1) + n, n % 2)

        @block.scalar
        def _(act):
            def sqrt_var(g):
                act.wait_ge(s.var_ready, g + 1)
                nc.scalar.activation(std[:, :], mv[:, :, 1], ACT.Sqrt).then_inc(s.std_ready, 1)

            def relu_tile(t, b):
                nc.scalar.activation(h_buf[:, b, :], x_slot[:, ds(t, 1), :].rearrange("p a n -> p (a n)"), ACT.Relu,
                                     bias=nmr[:, ds(t, 1)], scale=rstd[:, ds(t, 1)]).then_inc(s.h_ready, 1)

            def cast_adj(t, b):
                act.wait_ge(s.adj_in0 if b == 0 else s.adj_in1, x_loads(t, b))
                settle(act)
                nc.scalar.activation(adj_n8[:, ds(t, 1), :].rearrange("p a n -> p (a n)"), adj_in[:, b, :], ACT.Copy,
                                     scale=float(ONE8), accum_out=rowsum[:, ds(t, 1)]).then_inc(s.adj_cast, 1)

            def tiles(g, last):
                for k in range(G):
                    t = G * g + k
                    b = k % 2
                    if not (last and k == G - 1):
                        cast_adj(t + 1, 1 - b)
                    if not (last and k >= G - 2):
                        act.wait_ge(s.ln_ready, g + (1 if k < G - 2 else 2))
                        act.wait_ge(s.hT_ps, t + 3)
                        settle(act)
                        relu_tile(t + 2, b)
                    if k == 1 and not last:
                        sqrt_var(g + 1)
                    act.wait_ge(s.seq_ps, t + 1)
                    settle(act)
                    nc.scalar.activation(seq[:, ds(t, 1), :, 0:DH].rearrange("p a h c -> p (a h) c"),
                                         ps[:, 2 + b, :].rearrange("p (h c) -> p h c", c=DH), ACT.Copy)\
                        .then_inc(s.seq_sb, 1)
                    act.wait_ge(s.at_ps1, t + 3)
                    settle(act)
                    nc.scalar.activation(adj_t8[:, NT // 2:NT, ds(P * t, P)], ps_adj[1], ACT.Copy, scale=float(MINUS8))\
                        .then_inc(s.at_sb1, 1)

            start_rings(act, s.seq_sb, s.at_sb1)
            sqrt_var(0)
            act.wait_ge(s.ln_ready, 1)
            relu_tile(0, 0)
            relu_tile(1, 1)
            cast_adj(0, 0)
            with act.Fori(0, NG - 1) as g:
                tiles(g, False)
            tiles(NG - 1, True)

            act.wait_ge(s.small, 4)
            nc.scalar.activation(v2[:, :, 0, :], tdiff[:, :, :], ACT.Exp).then_inc(s.v_ready, 1)
            nc.scalar.activation(v2[:, :, 1, :], tdiff[:, :, :], ACT.Exp, scale=ALPHA).then_inc(s.v_ready, 1)
            act.wait_ge(s.small, 7)
            nc.scalar.activation(u2[:, :, 0, :], tmin[:, :, :], ACT.Exp, scale=1.0 - ALPHA).then_inc(s.u_ready, 1)
            nc.scalar.activation(u2[:, :, 1, :], tsum[:, :, :], ACT.Exp, scale=ALPHA - 1.0).then_inc(s.u_ready, 1)

            def head(h, b, hp):
                act.wait_ge(s.row_in0 if b == 0 else s.row_in1, 16 * hp + 32)
                act.wait_ge(s.bias_ready, h + 1)
                for c in range(NCH):
                    act.wait_ge(s.mask_used, NCH * h + c + 1)
                    settle(act)
                    for k in range(CJ):
                        jt = CJ * c + k
                        if jt not in DVE_JT:
                            step = nc.scalar.activation(mM[:, c % NSLOT, k, :], head_row[b], ACT.Sigmoid,
                                                        bias=kbias[:, b, jt:jt + 1], scale=BIG, saturate=False)
                    step.then_inc(s.steps, 1)

            with act.Fori(0, H // 2) as hp:
                for b in range(2):
                    head(2 * hp + b, b, hp)

            act.wait_ge(s.dinv_small, 4)
            nc.scalar.activation(dsum[:, :], colsum[:, :], ACT.Sqrt).then_inc(s.dinv_sqrt, 1)
            def pack_hidden(t, k):
                b = k % 2
                act.wait_ge(s.hid_ps, t + 1)
                settle(act)
                nc.scalar.activation(hid[:, b, :].rearrange("p (h c) -> p h c", c=DH),
                                     seq[:, ds(t, 1), :, 0:DH].rearrange("p a h c -> p (a h) c"), ACT.Copy)\
                    .then_inc(s.hid_cp, 1)

            def hidden_T(t, k):
                b = k % 2
                act.wait_ge(s.hid_ps, t + 3)
                act.wait_ge(s.o_ps, t + 1)
                nc.scalar.activation(hT2[:, b, :], ps[:, b, :], ACT.Copy).then_inc(s.hid_T, 1)

            def scaled_relu(t, b):
                act.wait_ge(s.glo, t + 1)
                settle(act)
                nc.scalar.activation(xb[:, b, :], x_slot[:, ds(t, 1), :].rearrange("p a n -> p (a n)"), ACT.Relu,
                                     bias=nmr[:, ds(t, 1)], scale=rstd[:, ds(t, 1)]).then_inc(s.xg_ready, 1)

            def sqrt2(g):
                act.wait_ge(s.ln2_var, g + 1)
                nc.scalar.activation(std[:, :], mv[:, :, 1], ACT.Sqrt).then_inc(s.ln2_std, 1)

            def out_group(g, first=False, last=False):
                for k in range(G):
                    b = k % 2
                    t = G * g + k
                    if not (last and k >= G - 2):
                        pack_hidden(t + 2, k)
                    if not (last and k == G - 1):
                        hidden_T(t + 1, k + 1)
                    act.wait_ge(s.t_ready, t + 3)
                    nc.scalar.activation(nbuf[:, b, :], tbuf[:, b, :], ACT.Exp).then_inc(s.e_ready, 1)
                    if k == 0 and not first:
                        sqrt2(g - 1)
                    if k == 1 and not first:
                        act.wait_ge(s.ln2_ready, g)
                    if not first:
                        for n in NORM_AT[k]:
                            scaled_relu(G * (g - 1) + n, n % 2)

            start_rings(act, s.hid_T, s.z_cp)
            act.wait_ge(s.hidden_ready, 2 * H - 1)
            pack_hidden(0, 0)
            pack_hidden(1, 1)
            hidden_T(0, 0)
            out_group(0, first=True)
            for n in range(4):
                act.wait_ge(s.ne_ps, n + 1)
                nc.scalar.activation(ne_row[:, n * 512:(n + 1) * 512], ps[:, 4 + n, :], ACT.Copy, saturate=False)\
                    .then_inc(s.ne_sb, 1)
            act.wait_ge(s.hidden_ready, 2 * H)
            with act.Fori(1, NG - 1) as g:
                out_group(g)
            out_group(NG - 1, last=True)
            sqrt2(NG - 1)
            act.wait_ge(s.ln2_ready, NG)
            for k in range(G):
                scaled_relu(NT - G + k, k % 2)
            with act.Fori(0, NT // 2) as i:
                for b in range(2):
                    t = 2 * i + b
                    act.wait_ge(s.z_ps, t + 3)
                    act.wait_ge(s.zlo, t + 1)
                    settle(act)
                    nc.scalar.activation(z_tmp[:, b, :], ps[:, b, :], ACT.Copy, scale=dsum[:, ds(t, 1)])\
                        .then_inc(s.z_cp, 1)

        @block.tensor
        def _(pe):
            def transpose_h(t, k):
                pe.wait_ge(s.h_ready, t + 1)
                for c in range(KC):
                    last = nc.tensor.transpose(ps[:, k % 2, c * P:(c + 1) * P], h_buf[:, k % 2, c * P:(c + 1) * P],
                                               ident[:, :])
                last.then_inc(s.hT_ps, 1)

            def tiles(g, last):
                for k in range(G):
                    t = G * g + k
                    b = k % 2
                    if not (last and k == G - 1):
                        transpose_h(t + 1, k + 1)
                    pe.wait_ge(s.hT_sb, t + 1)
                    if k == G - 1:
                        pe.wait_ge(s.wa_red, 2)
                        pe.wait_ge(s.sT_sb, g + 1)
                        settle(pe)
                        for n in range(G):
                            for c in range(KC):
                                mm = nc.tensor.matmul(ps[:, 6, n * 2 * H:(n + 1) * 2 * H],
                                                      hT[:, c, n * P:(n + 1) * P], w12[:, c, :],
                                                      start=(c == 0), stop=(c == KC - 1))
                        mm.then_inc(s.s12_ps, 1)
                    pe.wait_ge(s.seq_sb, t + 1)
                    for c in range(KC):
                        mm = nc.tensor.matmul(ps[:, 2 + b, :], hT[:, c, k * P:(k + 1) * P], wmat[:, c, :],
                                              start=(c == 0), stop=(c == KC - 1))
                    mm.then_inc(s.seq_ps, 1)
                    if k == G - 1:
                        pe.wait_ge(s.s12_sb, 2 * g + 2)
                        settle(pe)
                        for n in range(G):
                            st = nc.tensor.transpose(ps[0:2 * H, 6, n * P:(n + 1) * P], s_grp[:, n, :], ident[:, :])
                        st.then_inc(s.sT_ps, 1)
                    pe.wait_ge(s.adj_filled, t + 1)
                    for half in range(2):
                        pe.wait_ge((s.at_sb0, s.at_sb1)[half], t + 2)
                        for j in range(NT // 2):
                            jt = half * (NT // 2) + j
                            tr = nc.tensor.transpose(ps_adj[half][:, j, :], adj_b[:, b, jt * P:(jt + 1) * P],
                                                     ident_b[:, :])
                        if half == 0:
                            tr.then_inc(s.at_ps0, 1)
                    tr.then_inc(s.at_ps1, 1)
                    for j in range(NT):
                        mm = nc.tensor.matmul(ps[:, 7, j:j + 1],
                                              adj_b[:, b, j * P:(j + 1) * P],
                                              ones_b[:, 0:1], start=False, stop=False, skip_group_check=True)
                    mm.then_inc(s.adj_read, 1)

            start_rings(pe, s.hT_ps, s.at_ps1, s.adj_read)
            pe.wait_ge(s.consts, 6)
            nc.tensor.matmul(ps[:, 7, 0:NT], ones_b[:, :], zeros_b[:, :], start=True, stop=False,
                             skip_group_check=True)
            transpose_h(0, 0)
            pe.wait_ge(s.w_in, 16)
            with pe.Fori(0, NG - 1) as g:
                tiles(g, False)
            tiles(NG - 1, True)
            pe.wait_ge(s.small, 2)
            nc.tensor.matmul(ps[:, 6, 0:H], ones_f[:, :], dmax[:, H:2 * H], start=True, stop=True)\
                .then_inc(s.cmax_ps, 1)
            nc.tensor.matmul(ps[:, 6, H:H + NT], ones_p[:, :], empty[:, :], start=True, stop=True)\
                .then_inc(s.ne_cnt, 1)
            pe.wait_ge(s.small, 3)
            pe.wait_ge(s.dinv_small, 2)
            pe.sem_inc(s.mask_used, NSLOT)
            pe.sem_inc(s.acc_free, 2)

            def by_part(sums):
                return sums.rearrange("p (q s c) -> p q s c", q=NPART, s=2)

            def products(b, c, tiles, h):
                xor = c in XOR_CH

                def multiply(mask, sides, first, last):
                    for k in range(CJ):
                        jt = CJ * c + k
                        for t in tiles:
                            mm = nc.tensor.matmul(by_part(acc[:, t, :])[:, :, sides, :], mask(k, jt, t),
                                                  halves[:, b, :, jt, sides, :, 1],
                                                  start=(first and jt == 0 and t % 2 == 0),
                                                  stop=(last and jt == NT - 1),
                                                  skip_group_check=True)
                    return mm

                def columns(t):
                    return slice(t * P, (t + 1) * P)

                if not xor:
                    multiply(lambda k, jt, t: adj_t[:, jt, columns(t)], slice(1, 2), True, False)
                pe.wait_ge(s.m_ready, NCH * h + c + 1)
                settle(pe)
                mm = multiply(lambda k, jt, t: mM[:, c % NSLOT, k, columns(t)], slice(0, 1 if xor else 2), xor,
                              not xor)
                if xor:
                    pe.wait_ge(s.n_ready, len(XOR_CH) * h + len([x for x in XOR_CH if x < c]) + 1)
                    settle(pe)
                    mm = multiply(lambda k, jt, t: mN[:, c % NSLOT, k, columns(t)], slice(1, 2), False, True)
                return mm

            def head(h, b):
                pe.wait_ge(s.vals_ready, h + 1)
                for c in range(NCH):
                    if c not in (0, NCH - 1):
                        products(b, c, range(NT), h).then_inc(s.mask_used, 1)
                        continue
                    for half in range(2):
                        if c == 0:
                            pe.wait_ge(s.acc_free, 2 * h + half + 1)
                            settle(pe)
                        mm = products(b, c, range(half * TU, (half + 1) * TU), h)
                        if c == NCH - 1 and half == 0:
                            mm.then_inc(s.sums_half, 1)
                    mm.then_inc(s.mask_used, 1)

            with pe.Fori(0, H // 2) as hp:
                for b in range(2):
                    head(2 * hp + b, b)

            start_rings(pe, s.hid_ps, s.o_ps, s.z_ps, s.y_ps)
            pe.wait_ge(s.wo_in, 16)
            def transpose_hidden(t, k):
                pe.wait_ge(s.hid_cp, t + 1)
                pe.wait_ge(s.hid_T, t + 1)
                for c in range(KC):
                    tr = nc.tensor.transpose(ps[:, k % 2, c * P:(c + 1) * P], hid[:, k % 2, c * P:(c + 1) * P],
                                             ident[:, :])
                tr.then_inc(s.hid_ps, 1)

            def out_group(g, last):
                for k in range(G):
                    b = k % 2
                    t = G * g + k
                    if not (last and k == G - 1):
                        transpose_hidden(t + 1, k + 1)
                    pe.wait_ge(s.hid_T, t + 3)
                    pe.wait_ge(s.t_ready, t + 1)
                    for c in range(KC):
                        mm = nc.tensor.matmul(ps[:, 2 + b, :], hT2[:, b, c * P:(c + 1) * P], wmat[:, c, :],
                                              start=(c == 0), stop=(c == KC - 1))
                    mm.then_inc(s.o_ps, 1)

            transpose_hidden(0, 0)
            out_group(0, False)
            pe.wait_ge(s.acc_free, 2 * H + 2)
            pe.wait_ge(s.diag_ready, 1)
            for n in range(4):
                nc.tensor.matmul(ps[:, 4 + n, :], ones_b[:, :],
                                 diag.rearrange("p t c -> p (t c)")[:, n * 512:(n + 1) * 512],
                                 start=True, stop=True).then_inc(s.ne_ps, 1)
            with pe.Fori(1, NG - 1) as g:
                out_group(g, False)
            out_group(NG - 1, True)
            EARLY = NT - G - 2

            def z_products(b, jts, first=False):
                for jt in jts:
                    if first:
                        pe.wait_ge(s.glo, jt + 3)
                    for part in range(2):
                        mm = nc.tensor.matmul(ps[:, b, :], s_buf[:, b, jt, :], g_parts[:, jt, part, :],
                                              start=(jt == 0 and part == 0), stop=(jt == NT - 1 and part == 1))
                return mm

            def z_ready(t):
                pe.wait_ge(s.s_ready, t + 1)
                pe.wait_ge(s.z_cp, t + 1)

            for b in range(2):
                z_ready(b)
                z_products(b, range(EARLY), first=True)
            for b in range(2):
                z_products(b, range(EARLY, NT), first=True).then_inc(s.z_ps, 1)
            with pe.Fori(1, NT // 2) as i:
                for b in range(2):
                    z_ready(2 * i + b)
                    z_products(b, range(NT)).then_inc(s.z_ps, 1)
            with pe.Fori(0, NT // 2) as i:
                for b in range(2):
                    t = 2 * i + b
                    pe.wait_ge(s.a_ready, t + 1)
                    pe.wait_ge(s.y_sb, t + 1)
                    settle(pe)
                    for jt in range(NT):
                        pe.wait_ge(s.zlo, jt + 3)
                        for part in range(2):
                            mm = nc.tensor.matmul(ps[:, 2 + 2 * b + part, :], a_buf[:, b, jt, :],
                                                  z_parts[:, jt, part, :], start=(jt == 0), stop=(jt == NT - 1))
                    mm.then_inc(s.y_ps, 1)

        @block.vector
        def _(dve):
            def norm_stats(g):
                for k in range(G):
                    t = G * g + k
                    st = nc.vector.bn_stats(stats[:, k, :],
                                            x_slot[:, ds(t, 1), :].rearrange("p a n -> p (a n)"))
                st.then_inc(s.st_done, 1)
                dve.wait_ge(s.st_done, g + 1)
                settle(dve)
                for k in range(G):
                    ag = nc.vector.bn_aggr(mv[:, k, :], stats[:, k, :])
                ag.then_inc(s.ag_done, 1)
                dve.wait_ge(s.ag_done, g + 1)
                nc.vector.tensor_scalar(mv[:, :, 1], mv[:, :, 1], EPS, None, ALU.add).then_inc(s.var_ready, 1)

            def norm_scales(g):
                dve.wait_ge(s.std_ready, g + 1)
                settle(dve)
                nc.vector.reciprocal(rstd[:, ds(G * g, G)], std[:, :]).then_inc(s.rs_done, 1)
                dve.wait_ge(s.rs_done, g + 1)
                nc.vector.scalar_tensor_tensor(out=nmr[:, ds(G * g, G)], in0=mv[:, :, 0], scalar=-1.0,
                                               in1=rstd[:, ds(G * g, G)], op0=ALU.mult, op1=ALU.mult)\
                    .then_inc(s.ln_ready, 1)

            def copy_hT(t, k):
                dve.wait_ge(s.hT_ps, t + 3)
                nc.vector.tensor_copy(hT[:, :, (k % G) * P:(k % G + 1) * P],
                                      ps[:, k % 2, :].rearrange("p (c n) -> p c n", c=KC)).then_inc(s.hT_sb, 1)

            def fill_rows(t, b):
                dve.wait_ge(s.adj_cast, t + 1)
                nc.vector.tensor_scalar(empty[:, ds(t, 1)], rowsum[:, ds(t, 1)], 0.0, None, ALU.is_equal)\
                    .then_inc(s.empty_done, 1)
                dve.wait_ge(s.empty_done, t + 1)
                dve.wait_ge(s.adj_read, t + 1)
                nc.vector.tensor_scalar(adj_b[:, b, :], adj_n8[:, ds(t, 1), :].rearrange("p a n -> p (a n)"),
                                        1.0 / ONE8, empty[:, ds(t, 1)], ALU.mult, ALU.max).then_inc(s.adj_filled, 1)

            def sum_wa(n):
                dve.wait_ge(s.wa_mul, n + 1)
                nc.vector.reduce_sum(w12[:, :, n * H:(n + 1) * H], wa_tmp, AX_X).then_inc(s.wa_red, 1)

            def tiles(g, last, first=False):
                for k in range(G):
                    t = G * g + k
                    b = k % 2
                    if first and k < 2:
                        sum_wa(k)
                    if not (last and k == G - 1):
                        if k == G - 1:
                            dve.wait_ge(s.s12_ps, g + 1)
                            dve.wait_ge(s.seq_ps, t)
                            settle(dve)
                        copy_hT(t + 1, k + 1)
                        fill_rows(t + 1, 1 - b)
                    if k == G - 1:
                        dve.wait_ge(s.s12_ps, g + 1)
                        settle(dve)
                        nc.vector.tensor_copy(s_grp[:, :, :], ps[:, 6, 0:G * 2 * H].rearrange("p (t c) -> p t c", t=G))\
                            .then_inc(s.s12_sb, 1)
                        nc.vector.tensor_copy(s12[:, ds(G * g, G), :],
                                              ps[:, 6, 0:G * 2 * H].rearrange("p (t c) -> p t c", t=G))\
                            .then_inc(s.s12_sb, 1)
                        dve.wait_ge(s.sT_ps, g + 1)
                        nc.vector.tensor_copy(st_grp, ps[0:2 * H, 6, :]).then_inc(s.sT_sb, 1)
                        dve.wait_ge(s.sT_sb, g + 2)
                        nc.vector.tensor_scalar(st_rows[:, ds(G * P * g, G * P)].bitcast(U32), st_grp.bitcast(U32),
                                                0xFFFFFFFE, None, ALU.bitwise_and).then_inc(s.rows_sb, 1)
                        nc.vector.reduce_max(gmax[:, ds(g, 1)], st_grp, AX_X).then_inc(s.gmax_done, 1)
                    if k == 0 and not last:
                        norm_stats(g + 1)
                    if k == 1 and not last:
                        norm_scales(g + 1)
                    dve.wait_ge(s.at_ps0, t + 1)
                    nc.vector.tensor_scalar(adj_t8[:, 0:NT // 2, ds(P * t, P)], ps_adj[0], float(MINUS8), None,
                                            ALU.mult)\
                        .then_inc(s.at_sb0, 1)

            start_rings(dve, s.at_sb0)
            dve.sem_inc(s.sT_sb, 1)
            dve.wait_ge(s.x_first, 16)
            norm_stats(0)
            norm_scales(0)
            copy_hT(0, 0)
            fill_rows(0, 0)
            dve.wait_ge(s.x_second, 16)
            tiles(0, False, first=True)
            dve.wait_ge(s.x_rest, 16 * (NG - 2))
            with dve.Fori(1, NG - 1) as g:
                tiles(g, False)
            tiles(NG - 1, True)

            dve.wait_ge(s.gmax_done, NG)
            nc.vector.reduce_max(smax[:, :], gmax[:, :], AX_X).then_inc(s.small, 1)
            dve.wait_ge(s.s12_sb, 2 * NG)
            nc.vector.tensor_scalar(s2cmp[:, :, :], s12[:, :, H:2 * H], TINY, None, ALU.add).then_inc(s.cmp_ready, 1)
            dve.wait_ge(s.small, 1)
            nc.vector.tensor_scalar(dmax[:, :], ident[0:2 * H, 0:2 * H], smax[:, 0:1], None, ALU.mult)\
                .then_inc(s.small, 1)
            dve.wait_ge(s.cmp_ready, 1)
            nc.vector.tensor_scalar(s2cmp[:, :, :].bitcast(U32), s2cmp[:, :, :].bitcast(U32), 1, None, ALU.bitwise_or)\
                .then_inc(s.cmp_ready, 1)
            dve.wait_ge(s.cmp_ready, 2)
            nc.vector.tensor_scalar(kall[:, :, :], s2cmp[:, :, :], BIG, None, ALU.mult).then_inc(s.all_ready, 1)
            nc.vector.tensor_scalar(nall[:, :, :], s2cmp[:, :, :], -1.0, None, ALU.mult).then_inc(s.all_ready, 1)
            dve.wait_ge(s.cmax_ps, 1)
            dve.wait_ge(s.ne_cnt, 1)
            nc.vector.tensor_copy(cmax[:, :], ps[:, 6, 0:H]).then_inc(s.small, 1)
            dve.wait_ge(s.small, 3)
            c_all = cmax[:, :].unsqueeze(1).broadcast_to([P, NT, H])
            nc.vector.tensor_tensor(tdiff[:, :, :], s12[:, :, H:2 * H], c_all, ALU.subtract).then_inc(s.small, 1)
            nc.vector.tensor_tensor(tsum[:, :, :], s12[:, :, 0:H], c_all, ALU.add).then_inc(s.small, 1)

            def head_scalars(h, b):
                nc.vector.tensor_copy(kbias[:, b, :], kall[:, :, ds(h, 1)].rearrange("p t a -> p (t a)"))
                nc.vector.tensor_copy(negs2[:, b, :], nall[:, :, ds(h, 1)].rearrange("p t a -> p (t a)"))\
                    .then_inc(s.bias_ready, 1)

            def head_values(h, b):
                for side in range(2):
                    last = nc.vector.tensor_tensor(
                        parts[:, b, 0, :, side, :], seq[:, :, ds(h, 1), :].rearrange("p t a c -> p t (a c)"),
                        v2[:, :, side, ds(h, 1)].broadcast_to([P, NT, W33]), ALU.mult)
                last.then_inc(s.prep, 1)

            def head_rest(h, b, part):
                dve.wait_ge(s.prep, 2 * h + part)
                op = nc.vector.tensor_tensor(parts[:, b, part, :, :, :], parts[:, b, part - 1, :, :, :],
                                             halves[:, b, part - 1, :, :, :, 1], ALU.subtract)
                op.then_inc(s.prep if part == 1 else s.vals_ready, 1)

            dve.wait_ge(s.all_ready, 2)
            head_scalars(0, 0)
            dve.wait_ge(s.small, 5)
            nc.vector.tensor_scalar(tmin[:, :, :], tsum[:, :, :], 0.0, None, ALU.min).then_inc(s.small, 1)
            dve.wait_ge(s.small, 6)
            nc.vector.tensor_scalar(tsum[:, :, :], tsum[:, :, :], 0.0, None, ALU.max).then_inc(s.small, 1)
            nc.vector.reduce_sum(n_empty[:, :], ps[:, 6, H:H + NT], AX_X).then_inc(s.dinv_small, 1)
            dve.wait_ge(s.dinv_small, 1)
            dve.wait_ge(s.adj_read, NT + 2)
            nc.vector.tensor_scalar(colsum[:, :], ps[:, 7, 0:NT], n_empty[:, 0:1], None, ALU.subtract)\
                .then_inc(s.dinv_small, 1)
            dve.wait_ge(s.dinv_small, 2)
            dve.wait_ge(s.seq_sb, NT + 2)
            dve.wait_ge(s.ones_col, 1)
            dve.wait_ge(s.v_ready, 2)
            head_values(0, 0)
            head_rest(0, 0, 1)
            head_rest(0, 0, 2)
            nc.vector.scalar_tensor_tensor(out=colsum[:, :], in0=rowsum[:, :], scalar=1.0 / ONE8, in1=colsum[:, :],
                                           op0=ALU.mult, op1=ALU.add).then_inc(s.dinv_small, 1)
            dve.wait_ge(s.dinv_small, 3)
            nc.vector.tensor_scalar(colsum[:, :], colsum[:, :], 0.5, 1.0, ALU.mult, ALU.add).then_inc(s.dinv_small, 1)

            def head(h, b, hp, first, last):
                q = NCH * h

                def step(c):
                    for j in DVE_JT:
                        if j // CJ == c:
                            dve.wait_ge(s.mask_used, q + c + 1)
                            settle(dve)
                            nc.vector.tensor_scalar(mM[:, c % NSLOT, j % CJ, :], head_row[b], negs2[:, b, j:j + 1],
                                                    None, ALU.is_gt, saturate=False).then_inc(s.m_dve, 1)

                def chunk(c):
                    adj_c = adj_t[:, c * CJ:(c + 1) * CJ, :].bitcast(U32)
                    m_c = mM[:, c % NSLOT, :, :].bitcast(U32)
                    done = len([j for j in DVE_JT if j // CJ <= c])
                    if any(j // CJ == c for j in DVE_JT):
                        dve.wait_ge(s.m_dve, len(DVE_JT) * h + done)
                    dve.wait_ge(s.steps, q + c + 1)
                    nc.vector.tensor_tensor(m_c, m_c, adj_c, ALU.bitwise_and).then_inc(s.m_ready, 1)
                    if c < NCH - 1:
                        step(c + 1)
                    if c in XOR_CH:
                        dve.wait_ge(s.m_ready, q + c + 1)
                        nc.vector.tensor_tensor(mN[:, c % NSLOT, :, :].bitcast(U32), m_c, adj_c, ALU.bitwise_xor)\
                            .then_inc(s.n_ready, 1)

                dve.wait_ge(s.row_in0 if b == 0 else s.row_in1, 16 * hp + 32)
                dve.wait_ge(s.bias_ready, h + 1)
                step(0)
                for c in range(NCH):
                    chunk(c)
                    if not (first and b == 0):
                        if c == REDUCE_AT[0]:
                            reduce_half(h - 1, 0)
                        if c == REDUCE_AT[1]:
                            reduce_half(h - 1, 1)
                        if c == DIVIDE_AT[0]:
                            divide_half(h - 1, 0)
                        if c == DIVIDE_AT[1]:
                            divide_half(h - 1, 1)
                    if not last:
                        if c == 0:
                            head_scalars(h + 1, 1 - b)
                        if c == 3:
                            dve.wait_ge(s.mask_used, q + NSLOT)
                            dve.wait_ge(s.vals_ready, h + 1)
                            settle(dve)
                            head_values(h + 1, 1 - b)
                        if c == 4:
                            head_rest(h + 1, 1 - b, 1)
                        if c == 5:
                            head_rest(h + 1, 1 - b, 2)

            def reduce_half(h, half):
                if half == 0:
                    dve.wait_ge(s.sums_half, h + 1)
                else:
                    dve.wait_ge(s.mask_used, NCH * (h + 1) + NSLOT)
                if not isinstance(h, int) or h > 0:
                    dve.wait_ge(s.summed, 2 * h + half - 1)
                nc.vector.reduce_sum(red[:, half, :, :, :].rearrange("p t s c -> p t (s c)"),
                                     acc[:, half * TU:(half + 1) * TU, :].rearrange("p t (q c) -> p t c q", q=NPART),
                                     AX_X).then_inc(s.acc_free, 1)

            def divide_half(h, half):
                dve.wait_ge(s.summed, 2 * h + half + 1)
                nc.vector.reciprocal(rden[:, half, :], fin[:, :, DH]).then_inc(s.recip, 1)

            def pair_of_heads(hp, first=False, last=False):
                for b in range(2):
                    head(2 * hp + b, b, hp, first, last and b == 1)

            pair_of_heads(0, first=True)
            with dve.Fori(1, H // 2 - 1) as hp:
                pair_of_heads(hp)
            pair_of_heads(H // 2 - 1, last=True)
            reduce_half(H - 1, 0)
            start_rings(dve, s.t_ready)
            dve.wait_ge(s.mask_used, NSLOT)
            nc.vector.tensor_scalar(empty[:, :], empty[:, :], -1.0, 1.0, ALU.mult, ALU.add).then_inc(s.empty_done, 1)
            divide_half(H - 1, 0)
            reduce_half(H - 1, 1)
            divide_half(H - 1, 1)
            dve.wait_ge(s.empty_done, NT + 1)
            nc.vector.tensor_tensor(diag, ident_b[:, :].unsqueeze(1).broadcast_to([P, NT, P]),
                                    empty[:, :].unsqueeze(2).broadcast_to([P, NT, P]), ALU.mult)\
                .then_inc(s.diag_ready, 1)

            dve.wait_ge(s.dinv_sqrt, 1)
            nc.vector.reciprocal(dinv[:, :], dsum[:, :]).then_inc(s.dinv_ready, 1)
            dve.wait_ge(s.dinv_ready, 1)
            nc.vector.tensor_scalar(dsum[:, :], dinv[:, :], 0.5 * Z_SCALE * LO_SCALE / (G_SCALE * ONE8), None,
                                    ALU.mult)\
                .then_inc(s.dinv_ready, 1)

            def tile_of(buf, t):
                return buf[:, ds(t, 1), :].rearrange("p a n -> p (a n)")

            def norm2_scales(g):
                dve.wait_ge(s.ln2_std, g + 1)
                settle(dve)
                nc.vector.reciprocal(rstd[:, ds(G * g, G)], std[:, :]).then_inc(s.ln2_small, 1)
                dve.wait_ge(s.ln2_small, 2 * g + 1)
                nc.vector.scalar_tensor_tensor(out=rstd[:, ds(G * g, G)], in0=rstd[:, ds(G * g, G)], scalar=G_SCALE,
                                               in1=dinv[:, ds(G * g, G)], op0=ALU.mult, op1=ALU.mult)\
                    .then_inc(s.ln2_small, 1)
                dve.wait_ge(s.ln2_small, 2 * g + 2)
                nc.vector.scalar_tensor_tensor(out=nmr[:, ds(G * g, G)], in0=mv[:, :, 0], scalar=-1.0,
                                               in1=rstd[:, ds(G * g, G)], op0=ALU.mult, op1=ALU.mult)\
                    .then_inc(s.ln2_ready, 1)

            def high_part(t, b):
                dve.wait_ge(s.xg_ready, t + 1)
                nc.vector.tensor_copy(g_parts[:, ds(t, 1), 0, :].rearrange("p a n -> p (a n)"), xb[:, b, :])\
                    .then_inc(s.ghi, 1)

            ne_cols = ne_row.bitcast(U32)

            def true_columns(buf, t):
                return nc.vector.tensor_tensor(
                    buf, adj_t[:, :, :].bitcast(U32)[:, :, ds(P // 4 * t, P // 4)],
                    ne_cols[:, ds(P // 4 * t, P // 4)].unsqueeze(1).broadcast_to([P, NT, P // 4]), ALU.bitwise_and)

            def build_s(t, b):
                true_columns(col_buf.bitcast(U32), t).then_inc(s.col_true, 1)
                dve.wait_ge(s.col_true, t + 1)
                dve.wait_ge(s.z_ps, t + 1)
                nc.vector.tensor_tensor(s_buf[:, b, :, :], col_buf.bitcast(U8), adj_n8[:, :, ds(P * t, P)],
                                        ALU.add).then_inc(s.s_sum, 1)
                dve.wait_ge(s.s_sum, t + 1)
                nc.vector.scalar_tensor_tensor(out=tile_of(s_buf[:, b], t), in0=ident_b[:, :], scalar=2.0 * ONE8,
                                               in1=tile_of(s_buf[:, b], t), op0=ALU.mult, op1=ALU.add)\
                    .then_inc(s.s_ready, 1)

            def stats2(t, k):
                dve.wait_ge(s.x1_ready, t + 1)
                settle(dve)
                nc.vector.bn_stats(stats[:, k, :], tile_of(x_slot, t)).then_inc(s.ln2_st, 1)
                dve.wait_ge(s.ln2_st, t + 1)
                settle(dve)
                nc.vector.bn_aggr(mv[:, k, :], stats[:, k, :]).then_inc(s.ln2_ag, 1)

            def var2(g):
                dve.wait_ge(s.ln2_ag, G * g + G)
                nc.vector.tensor_scalar(mv[:, :, 1], mv[:, :, 1], EPS, None, ALU.add).then_inc(s.ln2_var, 1)

            def out_group(g, first=False, last=False):
                for k in range(G):
                    b = k % 2
                    t = G * g + k
                    dve.wait_ge(s.o_ps, t + 3)
                    nc.vector.tensor_tensor(tbuf[:, b, :], ps[:, 2 + b, :], b_row[:, :], ALU.add).then_inc(s.t_ready, 1)
                    if k == 1 and not first:
                        norm2_scales(g - 1)
                    if not (first and k == 0):
                        stats2(t - 1, (k - 1) % G)
                    if k == 0 and not first:
                        var2(g - 1)
                    dve.wait_ge(s.e_ready, t + 1)
                    nc.vector.tensor_scalar(nbuf[:, b, :], nbuf[:, b, :], 1.0, -1.0, ALU.min, ALU.add)\
                        .then_inc(s.em_ready, 1)
                    dve.wait_ge(s.em_ready, t + 1)
                    nc.vector.scalar_tensor_tensor(out=nbuf[:, b, :], in0=tbuf[:, b, :], scalar=0.0, in1=nbuf[:, b, :],
                                                   op0=ALU.max, op1=ALU.add).then_inc(s.q_ready, 1)
                    if not first:
                        for n in NORM_AT[k]:
                            high_part(G * (g - 1) + n, n % 2)
                    if last and k in (1, 2):
                        build_s(k - 1, k - 1)

            dve.wait_ge(s.b_in, 16)
            out_group(0, first=True)
            with dve.Fori(1, NG - 1) as g:
                out_group(g)
            dve.wait_ge(s.ne_sb, 4)
            out_group(NG - 1, last=True)
            stats2(NT - 1, G - 1)
            var2(NG - 1)
            norm2_scales(NG - 1)
            dve.wait_ge(s.glo, NT - G + 2)
            for k in range(G):
                t = NT - G + k
                high_part(t, k % 2)
                dve.wait_ge(s.ghi, t + 1)
                nc.vector.tensor_tensor(g_parts[:, t, 1, :], xb[:, k % 2, :], g_parts[:, t, 0, :], ALU.subtract)\
                    .then_inc(s.glo, 1)

            def copy_a(t, b):
                dve.wait_ge(s.y_ps, t + 1)
                true_columns(a_buf[:, b, :, :].bitcast(U32), t).then_inc(s.a_ready, 1)

            def split_z(t, b):
                dve.wait_ge(s.z_cp, t + 3)
                nc.vector.tensor_scalar(z_parts[:, ds(t, 1), 0, :].rearrange("p a n -> p (a n)"), z_tmp[:, b, :],
                                        1.0 / LO_SCALE, None, ALU.mult).then_inc(s.zhi, 1)
                dve.wait_ge(s.zhi, t + 1)
                nc.vector.scalar_tensor_tensor(out=z_parts[:, ds(t, 1), 1, :].rearrange("p a n -> p (a n)"),
                                               in0=z_parts[:, ds(t, 1), 0, :].rearrange("p a n -> p (a n)"),
                                               scalar=-LO_SCALE, in1=z_tmp[:, b, :], op0=ALU.mult, op1=ALU.add)\
                    .then_inc(s.zlo, 1)

            start_rings(dve, s.zlo, s.y_sb)
            with dve.Fori(0, NT // 2 - 1) as i:
                for b in range(2):
                    split_z(2 * i + b, b)
                    build_s(2 * i + b + 2, b)
            split_z(NT - 2, 0)
            dve.wait_ge(s.z_ps, NT + 1)
            copy_a(0, 0)
            split_z(NT - 1, 1)
            def finish_y(t, b, i):
                dve.wait_ge(s.y_ps, t + 3)
                dve.wait_ge((s.out_done0, s.out_done1)[b], 16 * i + 16)
                nc.vector.scalar_tensor_tensor(out=o_tmp[:, b, :], in0=ps[:, 2 + 2 * b, :], scalar=1.0 / Z_SCALE,
                                               in1=tile_of(x_slot, t), op0=ALU.mult, op1=ALU.add)\
                    .then_inc(s.y_hi, 1)
                dve.wait_ge(s.y_hi, t + 1)
                nc.vector.scalar_tensor_tensor(out=o_tmp[:, b, :], in0=ps[:, 3 + 2 * b, :],
                                               scalar=1.0 / (Z_SCALE * LO_SCALE), in1=o_tmp[:, b, :],
                                               op0=ALU.mult, op1=ALU.add).then_inc(s.y_sb, 1)

            with dve.Fori(0, NT // 2 - 1) as i:
                for b in range(2):
                    copy_a(2 * i + b + 1, 1 - b)
                    finish_y(2 * i + b, b, i)
            copy_a(NT - 1, 1)
            finish_y(NT - 2, 0, NT // 2 - 1)
            finish_y(NT - 1, 1, NT // 2 - 1)


_INS = ["x", "adj", "L0_gnn_W_seq", "L0_gnn_a1", "L0_gnn_a2", "L0_gnn_W_out", "L0_gnn_b_out"]


def kernel(**inputs):
    import numpy as np
    import concourse.bacc as bacc
    from concourse.bass_utils import run_bass_kernel_spmd

    nc = bacc.Bacc("TRN2", target_bir_lowering=False, num_devices=1)
    arrays, args = {}, []
    for name in _INS:
        a = np.ascontiguousarray(inputs[name])
        arrays[f"in_{name}"] = a
        args.append(nc.dram_tensor(f"in_{name}", a.shape, mybir.dt.from_np(a.dtype), kind="ExternalInput").ap())
    out = nc.dram_tensor("out", inputs["x"].shape, F32, kind="ExternalOutput").ap()
    gat_gcn(nc, *args, out)
    r = run_bass_kernel_spmd(nc, [arrays], core_ids=[0])
    return r.results[0]["out"]
```
